# Optimizing a Trainium2 kernel written in Bass

```python
import numpy as np
import jax
import jax.numpy as jnp

def _softmax(x, axis=-1):
    return jax.nn.softmax(x, axis=axis)

def _gelu(x):
    return jax.nn.gelu(x, approximate=True)

def _silu(x):
    return jax.nn.silu(x)

def _sigmoid(x):
    return jax.nn.sigmoid(x)

def _layernorm(x, axis=-1, eps=1e-05):
    m = jnp.mean(x, axis=axis, keepdims=True)
    v = jnp.var(x, axis=axis, keepdims=True)
    return (x - m) / jnp.sqrt(v + eps)

def _scatter_add(tgt, idx, src, axis=0):
    return tgt.at[idx].add(src)

def _segment_sum(src, seg, n):
    return jax.ops.segment_sum(src, seg, n)
kernel_name = 'mk_dlrm_tower_d1_rec_r8_5718ca'

def setup_inputs(seed: int=0):
    np.random.seed(seed)
    _w = jnp.asarray

    def _rec_inputs():
        import jax
        import jax.numpy as jnp
        _tk = jax.random.key(seed)
        dense_ctx = jax.random.normal(jax.random.fold_in(_tk, 190), (512, 16), jnp.float32)
        ids = jnp.stack([jax.random.randint(jax.random.fold_in(_tk, 200 + f), (512,), 0, v, jnp.int32) for f, v in enumerate([125000, 1000, 125000, 125000, 125000, 125000, 1250, 1250, 12500, 1250, 1000, 12500, 125000, 125000, 1000, 1250, 12500, 1000, 125000, 12500, 125000, 125000, 125000, 125000, 1000, 125000, 1000, 12500, 125000, 12500, 1250, 1250, 1000, 1250, 1250, 12500, 1250, 12500, 1250])], axis=1)
        tbl_0 = 0.05 * jax.random.normal(jax.random.fold_in(_tk, 500 + 0), (125000, 16), jnp.float32)
        tbl_1 = 0.05 * jax.random.normal(jax.random.fold_in(_tk, 500 + 1), (1000, 16), jnp.float32)
        tbl_2 = 0.05 * jax.random.normal(jax.random.fold_in(_tk, 500 + 2), (125000, 16), jnp.float32)
        tbl_3 = 0.05 * jax.random.normal(jax.random.fold_in(_tk, 500 + 3), (125000, 16), jnp.float32)
        tbl_4 = 0.05 * jax.random.normal(jax.random.fold_in(_tk, 500 + 4), (125000, 16), jnp.float32)
        tbl_5 = 0.05 * jax.random.normal(jax.random.fold_in(_tk, 500 + 5), (125000, 16), jnp.float32)
        tbl_6 = 0.05 * jax.random.normal(jax.random.fold_in(_tk, 500 + 6), (1250, 16), jnp.float32)
        tbl_7 = 0.05 * jax.random.normal(jax.random.fold_in(_tk, 500 + 7), (1250, 16), jnp.float32)
        tbl_8 = 0.05 * jax.random.normal(jax.random.fold_in(_tk, 500 + 8), (12500, 16), jnp.float32)
        tbl_9 = 0.05 * jax.random.normal(jax.random.fold_in(_tk, 500 + 9), (1250, 16), jnp.float32)
        tbl_10 = 0.05 * jax.random.normal(jax.random.fold_in(_tk, 500 + 10), (1000, 16), jnp.float32)
        tbl_11 = 0.05 * jax.random.normal(jax.random.fold_in(_tk, 500 + 11), (12500, 16), jnp.float32)
        tbl_12 = 0.05 * jax.random.normal(jax.random.fold_in(_tk, 500 + 12), (125000, 16), jnp.float32)
        tbl_13 = 0.05 * jax.random.normal(jax.random.fold_in(_tk, 500 + 13), (125000, 16), jnp.float32)
        tbl_14 = 0.05 * jax.random.normal(jax.random.fold_in(_tk, 500 + 14), (1000, 16), jnp.float32)
        tbl_15 = 0.05 * jax.random.normal(jax.random.fold_in(_tk, 500 + 15), (1250, 16), jnp.float32)
        tbl_16 = 0.05 * jax.random.normal(jax.random.fold_in(_tk, 500 + 16), (12500, 16), jnp.float32)
        tbl_17 = 0.05 * jax.random.normal(jax.random.fold_in(_tk, 500 + 17), (1000, 16), jnp.float32)
        tbl_18 = 0.05 * jax.random.normal(jax.random.fold_in(_tk, 500 + 18), (125000, 16), jnp.float32)
        tbl_19 = 0.05 * jax.random.normal(jax.random.fold_in(_tk, 500 + 19), (12500, 16), jnp.float32)
        tbl_20 = 0.05 * jax.random.normal(jax.random.fold_in(_tk, 500 + 20), (125000, 16), jnp.float32)
        tbl_21 = 0.05 * jax.random.normal(jax.random.fold_in(_tk, 500 + 21), (125000, 16), jnp.float32)
        tbl_22 = 0.05 * jax.random.normal(jax.random.fold_in(_tk, 500 + 22), (125000, 16), jnp.float32)
        tbl_23 = 0.05 * jax.random.normal(jax.random.fold_in(_tk, 500 + 23), (125000, 16), jnp.float32)
        tbl_24 = 0.05 * jax.random.normal(jax.random.fold_in(_tk, 500 + 24), (1000, 16), jnp.float32)
        tbl_25 = 0.05 * jax.random.normal(jax.random.fold_in(_tk, 500 + 25), (125000, 16), jnp.float32)
        tbl_26 = 0.05 * jax.random.normal(jax.random.fold_in(_tk, 500 + 26), (1000, 16), jnp.float32)
        tbl_27 = 0.05 * jax.random.normal(jax.random.fold_in(_tk, 500 + 27), (12500, 16), jnp.float32)
        tbl_28 = 0.05 * jax.random.normal(jax.random.fold_in(_tk, 500 + 28), (125000, 16), jnp.float32)
        tbl_29 = 0.05 * jax.random.normal(jax.random.fold_in(_tk, 500 + 29), (12500, 16), jnp.float32)
        tbl_30 = 0.05 * jax.random.normal(jax.random.fold_in(_tk, 500 + 30), (1250, 16), jnp.float32)
        tbl_31 = 0.05 * jax.random.normal(jax.random.fold_in(_tk, 500 + 31), (1250, 16), jnp.float32)
        tbl_32 = 0.05 * jax.random.normal(jax.random.fold_in(_tk, 500 + 32), (1000, 16), jnp.float32)
        tbl_33 = 0.05 * jax.random.normal(jax.random.fold_in(_tk, 500 + 33), (1250, 16), jnp.float32)
        tbl_34 = 0.05 * jax.random.normal(jax.random.fold_in(_tk, 500 + 34), (1250, 16), jnp.float32)
        tbl_35 = 0.05 * jax.random.normal(jax.random.fold_in(_tk, 500 + 35), (12500, 16), jnp.float32)
        tbl_36 = 0.05 * jax.random.normal(jax.random.fold_in(_tk, 500 + 36), (1250, 16), jnp.float32)
        tbl_37 = 0.05 * jax.random.normal(jax.random.fold_in(_tk, 500 + 37), (12500, 16), jnp.float32)
        tbl_38 = 0.05 * jax.random.normal(jax.random.fold_in(_tk, 500 + 38), (1250, 16), jnp.float32)
        _rk = jax.random.fold_in(_tk, 7)
        W_top1 = 0.05 * jax.random.normal(jax.random.fold_in(_tk, 801), (400, 512), jnp.float32)
        W_top2 = 0.0441942 * jax.random.normal(jax.random.fold_in(_tk, 802), (512, 256), jnp.float32)
        W_top3 = 0.0625 * jax.random.normal(jax.random.fold_in(_tk, 803), (256, 1), jnp.float32)
        b_top1 = jnp.zeros((512,), jnp.float32)
        b_top2 = jnp.zeros((256,), jnp.float32)
        return (dense_ctx, ids, tbl_0, tbl_1, tbl_2, tbl_3, tbl_4, tbl_5, tbl_6, tbl_7, tbl_8, tbl_9, tbl_10, tbl_11, tbl_12, tbl_13, tbl_14, tbl_15, tbl_16, tbl_17, tbl_18, tbl_19, tbl_20, tbl_21, tbl_22, tbl_23, tbl_24, tbl_25, tbl_26, tbl_27, tbl_28, tbl_29, tbl_30, tbl_31, tbl_32, tbl_33, tbl_34, tbl_35, tbl_36, tbl_37, tbl_38, W_top1, b_top1, W_top2, b_top2, W_top3)
    dense_ctx, ids, tbl_0, tbl_1, tbl_2, tbl_3, tbl_4, tbl_5, tbl_6, tbl_7, tbl_8, tbl_9, tbl_10, tbl_11, tbl_12, tbl_13, tbl_14, tbl_15, tbl_16, tbl_17, tbl_18, tbl_19, tbl_20, tbl_21, tbl_22, tbl_23, tbl_24, tbl_25, tbl_26, tbl_27, tbl_28, tbl_29, tbl_30, tbl_31, tbl_32, tbl_33, tbl_34, tbl_35, tbl_36, tbl_37, tbl_38, W_top1, b_top1, W_top2, b_top2, W_top3 = _rec_inputs()

    def _L0_rec_setup():
        import jax, jax.numpy as jnp
        import numpy as np
        B, F0, D = (512, 39, 16)
        CIN = [128, 128, 128]

        def _cin_layer(X0, Xi, W, b):
            H = W.shape[0]
            F0_, Fi = (X0.shape[1], Xi.shape[1])
            Wr = W.reshape(H, F0_, Fi)
            return jnp.einsum('hjk,bjd,bkd->bhd', Wr, X0, Xi) + b[None, :, None]
        key = jax.random.key(seed)
        ks = jax.random.split(key, 4)
        x = jax.random.normal(ks[0], (B, F0, D), dtype=jnp.float32)
        fields = [F0] + CIN
        inp = {'embedded_features': x}
        for i in range(len(CIN)):
            cin = F0 * fields[i]
            cout = fields[i + 1]
            kw = jax.random.fold_in(ks[1], i)
            inp[f'W{i}'] = jax.random.normal(kw, (cout, cin), dtype=jnp.float32) / np.sqrt(cin)
            inp[f'b{i}'] = jnp.zeros((cout,), dtype=jnp.float32)
        return inp
    _L0_rec_all = _L0_rec_setup()
    _L0_rec_in = {k: v for k, v in _L0_rec_all.items() if k in ('W0', 'b0', 'W1', 'b1', 'W2', 'b2')}
    del _L0_rec_all
    return {'dense_ctx': dense_ctx, 'ids': ids, 'tbl_0': tbl_0, 'tbl_1': tbl_1, 'tbl_2': tbl_2, 'tbl_3': tbl_3, 'tbl_4': tbl_4, 'tbl_5': tbl_5, 'tbl_6': tbl_6, 'tbl_7': tbl_7, 'tbl_8': tbl_8, 'tbl_9': tbl_9, 'tbl_10': tbl_10, 'tbl_11': tbl_11, 'tbl_12': tbl_12, 'tbl_13': tbl_13, 'tbl_14': tbl_14, 'tbl_15': tbl_15, 'tbl_16': tbl_16, 'tbl_17': tbl_17, 'tbl_18': tbl_18, 'tbl_19': tbl_19, 'tbl_20': tbl_20, 'tbl_21': tbl_21, 'tbl_22': tbl_22, 'tbl_23': tbl_23, 'tbl_24': tbl_24, 'tbl_25': tbl_25, 'tbl_26': tbl_26, 'tbl_27': tbl_27, 'tbl_28': tbl_28, 'tbl_29': tbl_29, 'tbl_30': tbl_30, 'tbl_31': tbl_31, 'tbl_32': tbl_32, 'tbl_33': tbl_33, 'tbl_34': tbl_34, 'tbl_35': tbl_35, 'tbl_36': tbl_36, 'tbl_37': tbl_37, 'tbl_38': tbl_38, 'W_top1': W_top1, 'b_top1': b_top1, 'W_top2': W_top2, 'b_top2': b_top2, 'W_top3': W_top3, 'L0_rec_W0': _L0_rec_in['W0'], 'L0_rec_b0': _L0_rec_in['b0'], 'L0_rec_W1': _L0_rec_in['W1'], 'L0_rec_b1': _L0_rec_in['b1'], 'L0_rec_W2': _L0_rec_in['W2'], 'L0_rec_b2': _L0_rec_in['b2']}

def reference(dense_ctx, ids, tbl_0, tbl_1, tbl_2, tbl_3, tbl_4, tbl_5, tbl_6, tbl_7, tbl_8, tbl_9, tbl_10, tbl_11, tbl_12, tbl_13, tbl_14, tbl_15, tbl_16, tbl_17, tbl_18, tbl_19, tbl_20, tbl_21, tbl_22, tbl_23, tbl_24, tbl_25, tbl_26, tbl_27, tbl_28, tbl_29, tbl_30, tbl_31, tbl_32, tbl_33, tbl_34, tbl_35, tbl_36, tbl_37, tbl_38, W_top1, b_top1, W_top2, b_top2, W_top3, L0_rec_W0, L0_rec_b0, L0_rec_W1, L0_rec_b1, L0_rec_W2, L0_rec_b2):
    import jax
    import jax.numpy as jnp

    def _L0_rec_ref(embedded_features, W0, b0, W1, b1, W2, b2):
        import jax, jax.numpy as jnp
        import numpy as np
        B, F0, D = (512, 39, 16)
        CIN = [128, 128, 128]

        def _cin_layer(X0, Xi, W, b):
            H = W.shape[0]
            F0_, Fi = (X0.shape[1], Xi.shape[1])
            Wr = W.reshape(H, F0_, Fi)
            return jnp.einsum('hjk,bjd,bkd->bhd', Wr, X0, Xi) + b[None, :, None]
        X0 = embedded_features
        Ws = [(W0, b0), (W1, b1), (W2, b2)]
        Xi = X0
        res = []
        for W, b in Ws:
            Xi = _cin_layer(X0, Xi, W, b)
            res.append(Xi.sum(axis=2))
        return jnp.concatenate(res, axis=1)
    e = jnp.stack([tbl_0[ids[:, 0]], tbl_1[ids[:, 1]], tbl_2[ids[:, 2]], tbl_3[ids[:, 3]], tbl_4[ids[:, 4]], tbl_5[ids[:, 5]], tbl_6[ids[:, 6]], tbl_7[ids[:, 7]], tbl_8[ids[:, 8]], tbl_9[ids[:, 9]], tbl_10[ids[:, 10]], tbl_11[ids[:, 11]], tbl_12[ids[:, 12]], tbl_13[ids[:, 13]], tbl_14[ids[:, 14]], tbl_15[ids[:, 15]], tbl_16[ids[:, 16]], tbl_17[ids[:, 17]], tbl_18[ids[:, 18]], tbl_19[ids[:, 19]], tbl_20[ids[:, 20]], tbl_21[ids[:, 21]], tbl_22[ids[:, 22]], tbl_23[ids[:, 23]], tbl_24[ids[:, 24]], tbl_25[ids[:, 25]], tbl_26[ids[:, 26]], tbl_27[ids[:, 27]], tbl_28[ids[:, 28]], tbl_29[ids[:, 29]], tbl_30[ids[:, 30]], tbl_31[ids[:, 31]], tbl_32[ids[:, 32]], tbl_33[ids[:, 33]], tbl_34[ids[:, 34]], tbl_35[ids[:, 35]], tbl_36[ids[:, 36]], tbl_37[ids[:, 37]], tbl_38[ids[:, 38]]], axis=1)
    z = _L0_rec_ref(e, L0_rec_W0, L0_rec_b0, L0_rec_W1, L0_rec_b1, L0_rec_W2, L0_rec_b2)
    z = z.reshape(z.shape[0], -1)
    h = jnp.concatenate([z, dense_ctx], axis=1)
    h = jnp.maximum(h @ W_top1 + b_top1, 0.0)
    h = jnp.maximum(h @ W_top2 + b_top2, 0.0)
    y = h @ W_top3
    return y

_drawn_inputs = setup_inputs


def setup_inputs(seed=0):
    import zlib

    import numpy as np

    out = dict(_drawn_inputs(seed))
    spreads = {'b_top1': (0.0, 0.1),
     'b_top2': (0.0, 0.1),
     'L0_rec_b0': (0.0, 0.1),
     'L0_rec_b1': (0.0, 0.1),
     'L0_rec_b2': (0.0, 0.1)}
    factors = {'tbl_0': 8.0,
     'tbl_1': 5.783,
     'tbl_2': 5.268,
     'tbl_3': 7.325,
     'tbl_4': 8.0,
     'tbl_5': 8.0,
     'tbl_6': 8.0,
     'tbl_7': 6.969,
     'tbl_8': 8.0,
     'tbl_9': 8.0,
     'tbl_10': 8.0,
     'tbl_11': 6.264,
     'tbl_12': 8.0,
     'tbl_13': 8.0,
     'tbl_14': 4.346,
     'tbl_15': 5.815,
     'tbl_16': 8.0,
     'tbl_17': 8.0,
     'tbl_18': 8.0,
     'tbl_19': 5.996,
     'tbl_20': 7.152,
     'tbl_21': 8.0,
     'tbl_22': 8.0,
     'tbl_23': 8.0,
     'tbl_24': 8.0,
     'tbl_25': 7.407,
     'tbl_26': 5.749,
     'tbl_27': 8.0,
     'tbl_28': 8.0,
     'tbl_29': 8.0,
     'tbl_30': 6.908,
     'tbl_31': 5.989,
     'tbl_32': 8.0,
     'tbl_33': 6.941,
     'tbl_34': 8.0,
     'tbl_35': 6.936,
     'tbl_36': 8.0,
     'tbl_37': 6.768,
     'tbl_38': 8.0,
     'L0_rec_W0': 3.231}
    for name, (base, spread) in spreads.items():
        noise = np.random.default_rng([zlib.crc32(name.encode()), seed]).standard_normal(out[name].shape)
        drawn = base * np.exp(spread * noise) if base else spread * noise
        out[name] = jnp.asarray(drawn.astype(out[name].dtype))
    for name, factor in factors.items():
        out[name] = (out[name] * factor).astype(out[name].dtype)
    return out
```

```python
from contextlib import ExitStack

import numpy as np
import concourse.bass as bass
from concourse import mybir

ALU = mybir.AluOpType
ACT = mybir.ActivationFunctionType
AX_X = mybir.AxisListType.X
F32 = mybir.dt.float32
F32R = mybir.dt.float32r
I32 = mybir.dt.int32

P = 128
B, F, D = 512, 39, 16
H = 128
NDELTA = (F + 1) // 2
PER_CHUNK = 3
PAIR_CHUNKS = -(-NDELTA // PER_CHUNK)
PAIRS = PER_CHUNK * F
LO = 64
XROWS = LO + F
BLOCK_B = 32
NBLOCKS = B // BLOCK_B
COLS = BLOCK_B * D
TILE_B = P // D
TILES = COLS // P
BTILES = B // P
FE = F + 1
JC = 4
CHUNKS = -(-F // JC)
SLOTS = TILES * CHUNKS
VBANKS = 4
FIELDS = [list(range(c * JC, min(c * JC + JC, F))) for c in range(CHUNKS)]

ACT_CHUNKS = [1, 4, 6, 9]
DVE_CHUNKS = [c for c in range(CHUNKS) if c not in ACT_CHUNKS]
STT_TILE = sum(len(FIELDS[c]) for c in DVE_CHUNKS) + 1
MUL_TILE = sum(len(FIELDS[c]) for c in ACT_CHUNKS)
NSUM = len(ACT_CHUNKS)
POOL_TILE = NSUM + 2
POOL_BLOCK = TILES * (1 + POOL_TILE)
SIDE = 3 + PAIR_CHUNKS

S_SPLIT, S_TURN, S_TURNED, S_REP, S_REPPED = 0, 4, 5, 7, 9
S_PAIR, S_QUAD, S_L0 = 10, 11, 13
S_X1 = 33
X1_PARTS = [(0, COLS - P), (COLS - P, COLS)]
LAG_G2, LAG_G2E = 5, 7

NBIAS = 11
GATHERED_FIRST = F + 15


def bass_dlrm(nc, ids, tables, dense, w_top1, b_top1, w_top2, b_top2, w_top3,
              w0, b0, w1, b1, w2, b2, ident_c, sel_c, mask_c, y):
    ctx = ExitStack()
    with ctx:
        def sb(name, shape, dt=F32, stack=ctx):
            return stack.enter_context(nc.sbuf_tensor(name, shape, dt))

        def sem(name):
            return ctx.enter_context(nc.semaphore(name))

        early = ExitStack()
        w0_raw = sb("w0_raw", [P, F * F], F32, early)
        w0_sym = sb("w0_sym", [P, NDELTA, F], F32, early)
        w1_raw = sb("w1_raw", [P, F * H], F32, early)
        w2_raw = sb("w2_raw", [P, F * H], F32, early)
        sel_raw = sb("sel_raw", [XROWS, (PAIR_CHUNKS + 1) * PAIRS + FE], F32, early)
        dense_raw = sb("dense_raw", [P, BTILES, D], F32, early)
        early.close()
        g2 = sb("g2", [P, FE, B])

        middle = ExitStack()
        w1_hi = sb("w1_hi", [P, F * H], F32R, middle)
        w1_lo = sb("w1_lo", [P, F * H], F32R, middle)
        middle.close()
        late = ExitStack()
        wt1 = sb("wt1", [P, 3, 512], F32, late)
        wt1_dense = sb("wt1_dense", [D, 512], F32, late)
        wt2 = sb("wt2", [P, 4, 256], F32, late)
        h1 = sb("h1", [P, 4, B], F32, late)
        h2 = sb("h2", [P, 2, B], F32, late)
        z3 = sb("z3", [P, B], F32, late)
        y_row = sb("y_row", [1, B], F32, late)
        late.close()
        middle_again = sb("w1_place", [P, 2 * F * H])
        del middle_again

        ids_sb = sb("ids_sb", [P, BTILES, F], I32)
        emb = sb("emb", [P, BTILES, F * D])
        emb_block = sb("emb_block", [BLOCK_B, F * D])
        emb_parts = sb("emb_parts", [BLOCK_B, D, XROWS], F32R)
        ident = sb("ident", [P, P])
        ident_r = sb("ident_r", [BLOCK_B, BLOCK_B], F32R)
        mask = sb("mask", [P, TILE_B])
        sel = sb("sel", [XROWS, (PAIR_CHUNKS + 1) * PAIRS + FE], F32R)
        w0_t = sb("w0_t", [PAIRS, PAIR_CHUNKS, H])
        w2_t = sb("w2_t", [P, F * H])
        x0 = sb("x0", [XROWS, COLS], F32R)
        x0_rep = sb("x0_rep", [PAIRS, COLS])
        quad = sb("quad", [PAIRS, 2, COLS])
        x0_t_next = sb("x0_t_next", [P, TILES, F])
        x0_t = sb("x0_t", [P, TILES, FE])
        x1 = sb("x1", [P, COLS])
        x1_hi = sb("x1_hi", [P, COLS], F32R)
        x1_lo = sb("x1_lo", [P, COLS], F32R)
        acc = sb("acc", [P, 2, 2, H])
        prod = sb("prod", [P, NSUM, JC * H])
        part = sb("part", [P, JC * H])
        x2_t = sb("x2_t", [P, 2, H])
        spread = sb("spread", [P, TILES, TILE_B * FE])
        b0_sb = sb("b0_sb", [P, 1])
        b1_row = sb("b1_row", [P, H])
        b2_sb = sb("b2_sb", [P, 1])
        b2_x16 = sb("b2_x16", [P, 1])
        bt1_sb = sb("bt1_sb", [P, 4])
        bt2_sb = sb("bt2_sb", [P, 2])
        wt3 = sb("wt3", [P, 2])
        dense_t = sb("dense_t", [D, B])
        z1 = sb("z1", [P, B])

        v = ctx.enter_context(nc.psum_tensor("v", [P, VBANKS, 512], F32))
        side = ctx.enter_context(nc.psum_tensor("side", [P, 2, 512], F32))
        x1_ps = ctx.enter_context(nc.psum_tensor("x1_ps", [P, COLS], F32))
        g2_ps = ctx.enter_context(nc.psum_tensor("g2_ps", [P, 512], F32))

        sel_rep = sel[:, 0:PAIRS]
        sel_fields = sel[:, (PAIR_CHUNKS + 1) * PAIRS:]

        def sel_pair(c):
            return sel[:, (1 + c) * PAIRS:(1 + c) * PAIRS + pairs(c)]

        def pairs(c):
            return min(PER_CHUNK, NDELTA - PER_CHUNK * c) * F

        s_ids, s_w0, s_w1, s_w2 = sem("s_ids"), sem("s_w0"), sem("s_w1"), sem("s_w2")
        s_const, s_bias, s_dense = sem("s_const"), sem("s_bias"), sem("s_dense")
        s_gathered = [sem(f"s_gathered{t}") for t in range(BTILES)]
        s_block = sem("s_block")
        s_top = sem("s_top")
        s_out = sem("s_out")
        s_zeroed = sem("s_zeroed")
        s_sym = sem("s_sym")
        s_sel = sem("s_sel")
        s_tr = sem("s_tr")
        s_tr_hi = sem("s_tr_hi")
        s_tr_lo = sem("s_tr_lo")
        s_scaled = sem("s_scaled")
        s_hi = sem("s_hi")
        s_lo = sem("s_lo")
        s_side = sem("s_side")
        s_x0 = sem("s_x0")
        s_rep = sem("s_rep")
        s_x0t = sem("s_x0t")
        s_quad = sem("s_quad")
        s_l0 = sem("s_l0")
        s_x1 = sem("s_x1")
        s_x1h = sem("s_x1h")
        s_x1l = sem("s_x1l")
        s_z1 = sem("s_z1")
        s_cur = sem("s_cur")
        s_v = sem("s_v")
        s_stt = sem("s_stt")
        s_mul = sem("s_mul")
        s_pool = sem("s_pool")
        s_g2 = sem("s_g2")
        s_g2e = sem("s_g2e")
        s_z3 = sem("s_z3")
        s_z3e = sem("s_z3e")
        s_m1, s_m1e = sem("s_m1"), sem("s_m1e")
        s_m2, s_m2e = sem("s_m2"), sem("s_m2e")
        s_y, s_ye = sem("s_y"), sem("s_ye")

        W1_GROUP0 = 4
        W2_GROUP0 = W1_GROUP0 + CHUNKS
        GROUPS = W2_GROUP0 + CHUNKS

        def stt_done(g):
            t, c = divmod(g, CHUNKS)
            return STT_TILE * t + sum(len(FIELDS[x]) for x in DVE_CHUNKS if x <= c)

        def mul_done(g):
            t, c = divmod(g, CHUNKS)
            return MUL_TILE * t + sum(len(FIELDS[x]) for x in ACT_CHUNKS if x <= c)

        def pool_done(t, step):
            return TILES + POOL_TILE * t + step

        block = ctx.enter_context(nc.Block())

        @block.sync
        def _(sp):
            sp.dma_start(ids_sb[:, :, :], ids.rearrange("(t p) f -> p t f", p=P)).then_inc(s_ids, 16)
            sp.dma_start(w0_raw[:, :], w0).then_inc(s_w0, 16)
            sp.dma_start(ident[:, :], ident_c).then_inc(s_const, 16)
            sp.dma_start(sel_raw[:, :], sel_c).then_inc(s_const, 16)
            sp.dma_start(mask[:, :], mask_c).then_inc(s_const, 16)
            sp.dma_start(w1_raw[:, :], w1).then_inc(s_w1, 16)
            sp.dma_start(dense_raw[:, :, :], dense.rearrange("(t p) f -> p t f", p=P)).then_inc(s_dense, 16)
            sp.dma_start(b0_sb[:, :], b0.rearrange("(h o) -> h o", o=1)).then_inc(s_bias, 16)
            sp.dma_start(b2_sb[:, :], b2.rearrange("(h o) -> h o", o=1)).then_inc(s_bias, 16)
            sp.dma_start(b1_row[:, :], b1.rearrange("(o h) -> o h", o=1).broadcast_to([P, H])).then_inc(s_bias, 16)
            for c in range(4):
                sp.dma_start(bt1_sb[:, c:c + 1], b_top1[c * P:(c + 1) * P].rearrange("(h o) -> h o", o=1)).then_inc(s_bias, 16)
            for c in range(2):
                sp.dma_start(bt2_sb[:, c:c + 1], b_top2[c * P:(c + 1) * P].rearrange("(h o) -> h o", o=1)).then_inc(s_bias, 16)
                sp.dma_start(wt3[:, c:c + 1], w_top3[c * P:(c + 1) * P, :]).then_inc(s_bias, 16)
            sp.dma_start(w2_raw[:, :], w2).then_inc(s_w2, 16)
            for m in range(NBLOCKS):
                t, q = divmod(m, P // BLOCK_B)
                if q == 0:
                    sp.wait_ge(s_gathered[t], 16 * F)
                if m >= 1:
                    sp.wait_ge(s_lo, m)
                sp.dma_start(emb_block[:, :], emb[q * BLOCK_B:(q + 1) * BLOCK_B, t, :]).then_inc(s_block, 16)
            sp.wait_ge(s_v, SLOTS * NBLOCKS)
            sp.dma_start(wt1[:, :, :], w_top1[0:3 * P, :].rearrange("(c p) m -> p c m", p=P)).then_inc(s_top, 16)
            sp.dma_start(wt1_dense[:, :], w_top1[3 * P:3 * P + D, :]).then_inc(s_top, 16)
            sp.dma_start(wt2[:, :, :], w_top2.rearrange("(c p) m -> p c m", p=P)).then_inc(s_top, 16)
            sp.wait_ge(s_ye, 1)
            sp.dma_start(y.rearrange("b o -> o b"), y_row[:, :]).then_inc(s_out, 16)
            sp.wait_ge(s_out, 16)

        @block.gpsimd
        def _(pool):
            order = [(t, j) for t in range(BTILES) for j in range(F)]

            def gather(n):
                for t, j in order[:n]:
                    nc.gpsimd.indirect_dma_start(
                        emb[:, t, j * D:(j + 1) * D], None, tables[j],
                        bass.IndirectOffsetOnAxis(ids_sb[:, t, j:j + 1], 0)).then_inc(s_gathered[t], 16)
                del order[:n]

            def spread_x0(n, t, first):
                if t == 0:
                    pool.wait_ge(s_cur, n + 1)
                if not first:
                    pool.wait_ge(s_g2, n * TILES + t + 1 - TILES)
                nc.gpsimd.tensor_tensor(
                    spread[:, t, :].rearrange("p (b j) -> p b j", b=TILE_B),
                    mask[:, :].unsqueeze(2).broadcast_to([P, TILE_B, FE]),
                    x0_t[:, t, :].unsqueeze(1).broadcast_to([P, TILE_B, FE]), ALU.mult).then_inc(s_pool, 1)

            def sum_tile(n, t, first):
                base, muls = n * POOL_BLOCK, n * (TILES * MUL_TILE)
                for k in range(1, NSUM):
                    w = len(FIELDS[ACT_CHUNKS[k]]) * H
                    pool.wait_ge(s_mul, muls + mul_done(t * CHUNKS + ACT_CHUNKS[k]))
                    pool.wait_ge(s_pool, base + pool_done(t, k - 1))
                    nc.gpsimd.tensor_tensor(part[:, 0:w], prod[:, 0, 0:w] if k == 1 else part[:, 0:w],
                                            prod[:, k, 0:w], ALU.add).then_inc(s_pool, 1)
                pool.wait_ge(s_pool, base + pool_done(t, NSUM - 1))
                nc.gpsimd.tensor_tensor(part[:, 0:2 * H], part[:, 0:2 * H], part[:, 2 * H:4 * H],
                                        ALU.add).then_inc(s_pool, 1)
                pool.wait_ge(s_pool, base + pool_done(t, NSUM))
                nc.gpsimd.tensor_tensor(part[:, 0:H], part[:, 0:H], part[:, H:2 * H], ALU.add).then_inc(s_pool, 1)
                pool.wait_ge(s_pool, base + pool_done(t, NSUM + 1))
                pool.wait_ge(s_stt, n * (TILES * STT_TILE) + STT_TILE * (t + 1))
                if not (first and t < 2):
                    pool.wait_ge(s_g2, n * TILES + t - 1)
                nc.gpsimd.tensor_tensor(x2_t[:, t % 2, :], part[:, 0:H], acc[:, t % 2, 0, :],
                                        ALU.add).then_inc(s_pool, 1)

            pool.wait_ge(s_ids, 16)
            gather(GATHERED_FIRST)
            pool.wait_ge(s_const, 48)
            n, turn = 0, 0
            while order:
                for t in range(TILES):
                    spread_x0(n, t, n == 0)
                for t in range(TILES):
                    sum_tile(n, t, n == 0)
                    gather(2 + turn % 2)
                    turn += 1
                n += 1
            with pool.Fori(n, NBLOCKS) as i:
                for t in range(TILES):
                    spread_x0(i, t, False)
                for t in range(TILES):
                    sum_tile(i, t, False)

        @block.scalar
        def _(act):
            def split_hi(m, first):
                act.wait_ge(s_block, 16 * (m + 1))
                if first:
                    act.wait_ge(s_zeroed, 2)
                else:
                    act.wait_ge(s_side, SIDE * m - SIDE + 1)
                nc.scalar.activation(emb_parts[:, :, 0:F], emb_block[:, :].rearrange("b (j d) -> b d j", d=D),
                                     ACT.Copy).then_inc(s_hi, 1)

            def copy_x0(m):
                act.wait_ge(s_side, SIDE * m + 1)
                nc.scalar.activation(x0[:, :].rearrange("p (b d) -> p d b", d=D),
                                     side[0:XROWS, 0, :].rearrange("p (d b) -> p d b", d=D),
                                     ACT.Copy).then_inc(s_x0, 1)

            def copy_rep(m, first):
                act.wait_ge(s_side, SIDE * m + 2)
                if not first:
                    act.wait_ge(s_quad, PAIR_CHUNKS * m)
                nc.scalar.activation(x0_rep[:, :], side[0:PAIRS, 1, :], ACT.Copy).then_inc(s_rep, 1)

            def copy_x1(m, first):
                act.wait_ge(s_l0, PAIR_CHUNKS * (m + 1))
                if not first:
                    act.wait_ge(s_x1l, 2 * m)
                    act.wait_ge(s_z1, m)
                nc.scalar.activation(x1[:, :], x1_ps[:, :], ACT.Identity, bias=b0_sb[:, 0:1]).then_inc(s_x1, 1)

            def x1_split_hi(m, part, first):
                a, b = X1_PARTS[part]
                act.wait_ge(s_x1, m + 1)
                if not first:
                    act.wait_ge(s_v, SLOTS * m - SLOTS + CHUNKS * (b // P))
                nc.scalar.activation(x1_hi[:, a:b], x1[:, a:b], ACT.Copy).then_inc(s_x1h, 1)

            def products(n, g, first):
                t, c = divmod(g, CHUNKS)
                k = ACT_CHUNKS.index(c)
                if g == ACT_CHUNKS[0]:
                    act.wait_ge(s_cur, n + 1)
                if not (first and t == 0):
                    before = max(k, 1)
                    act.wait_ge(s_pool, n * POOL_BLOCK + (pool_done(t - 1, before) if t else
                                                          pool_done(TILES - 1, before) - POOL_BLOCK))
                act.wait_ge(s_v, n * SLOTS + g + 1)
                for x, j in enumerate(FIELDS[c]):
                    nc.scalar.activation(prod[:, k, x * H:(x + 1) * H], v[:, g % VBANKS, x * H:(x + 1) * H],
                                         ACT.Copy, scale=x0_t[:, t, j:j + 1]).then_inc(s_mul, 1)

            def copy_g2(n, t):
                b_at = n * BLOCK_B + t * TILE_B
                act.wait_ge(s_g2, n * TILES + t + 1)
                act.wait_ge(s_tr_hi, GROUPS)
                nc.scalar.activation(g2[:, :, bass.ds(b_at, TILE_B)],
                                     g2_ps[:, 0:TILE_B * FE].rearrange("p (b j) -> p j b", b=TILE_B),
                                     ACT.Copy).then_inc(s_g2e, 1)

            def step(n, first=False, last=False):
                for g in range(SLOTS):
                    if g == 0 and not first:
                        x1_split_hi(n, 1, False)
                    if not last:
                        m = n + 1
                        if g == S_SPLIT:
                            split_hi(m, False)
                        if g == S_TURNED:
                            copy_x0(m)
                        if g == S_REPPED:
                            copy_rep(m, False)
                        if g == S_X1:
                            copy_x1(m, False)
                            x1_split_hi(m, 0, False)
                    t, lag = divmod(g - LAG_G2E, CHUNKS)
                    if lag == 0 and t >= 1:
                        copy_g2(n, t - 1)
                    if lag == 0 and t == 0 and not first:
                        copy_g2(n - 1, TILES - 1)
                    if g % CHUNKS in ACT_CHUNKS:
                        products(n, g, first)

            act.wait_ge(s_const, 48)
            nc.scalar.activation(sel[:, :], sel_raw[:, :], ACT.Copy).then_inc(s_sel, 1)
            nc.scalar.activation(ident_r[:, :], ident[0:BLOCK_B, 0:BLOCK_B], ACT.Copy).then_inc(s_sel, 1)
            for s in range(GROUPS):
                act.wait_ge(s_tr, s + 1)
                bank = v[:, s % VBANKS, :]
                if s < 3:
                    rows, c0, c1 = [(PAIRS, 0, 4), (PAIRS, 4, 6), (pairs(6), 6, 7)][s]
                    nc.scalar.activation(w0_t[0:rows, c0:c1, :].rearrange("p c h -> p (c h)"),
                                         bank[0:rows, 0:(c1 - c0) * H], ACT.Copy).then_inc(s_tr_hi, 1)
                elif s == 3:
                    nc.scalar.activation(dense_t[:, :], bank[0:D, :], ACT.Copy).then_inc(s_tr_hi, 1)
                else:
                    dst, c = (w1_hi, s - W1_GROUP0) if s < W2_GROUP0 else (w2_t, s - W2_GROUP0)
                    w = len(FIELDS[c]) * H
                    nc.scalar.activation(dst[:, c * JC * H:c * JC * H + w], bank[:, 0:w], ACT.Copy).then_inc(s_tr_hi, 1)
            act.wait_ge(s_bias, 16 * NBIAS)
            nc.scalar.mul(b2_x16[:, :], b2_sb[:, :], float(D)).then_inc(s_scaled, 1)
            split_hi(0, True)
            copy_x0(0)
            copy_rep(0, True)
            copy_x1(0, True)
            for part in range(2):
                x1_split_hi(0, part, True)
            step(0, first=True)
            with act.Fori(1, NBLOCKS - 1) as i:
                step(i)
            step(NBLOCKS - 1, last=True)
            copy_g2(NBLOCKS - 1, TILES - 1)
            act.wait_ge(s_scaled, 1)
            act.wait_ge(s_z3, 1)
            nc.scalar.activation(z3[:, :], v[:, 0, :], ACT.Identity, bias=b2_x16[:, 0:1]).then_inc(s_z3e, 1)
            for c in range(4):
                act.wait_ge(s_m1, c + 1)
                nc.scalar.activation(h1[:, c, :], side[:, c % 2, :], ACT.Relu, bias=bt1_sb[:, c:c + 1]).then_inc(s_m1e, 1)
            for c in range(2):
                act.wait_ge(s_m2, c + 1)
                nc.scalar.activation(h2[:, c, :], v[:, 1 + c, :], ACT.Relu, bias=bt2_sb[:, c:c + 1]).then_inc(s_m2e, 1)
            act.wait_ge(s_y, 1)
            nc.scalar.activation(y_row[:, :], x1_ps[0:1, :], ACT.Copy).then_inc(s_ye, 1)

        @block.vector
        def _(dve):
            def split_lo(m):
                dve.wait_ge(s_hi, m + 1)
                nc.vector.tensor_tensor(emb_parts[:, :, LO:LO + F], emb_block[:, :].rearrange("b (j d) -> b d j", d=D),
                                        emb_parts[:, :, 0:F].bitcast(F32), ALU.subtract).then_inc(s_lo, 1)

            def copy_x0_t(m, first):
                dve.wait_ge(s_side, SIDE * m + 3)
                if not first:
                    dve.wait_ge(s_cur, m)
                nc.vector.tensor_copy(x0_t_next[:, :, :],
                                      side[:, 0, 0:TILES * FE].rearrange("p (t j) -> p t j", j=FE)[:, :, 0:F]
                                      ).then_inc(s_x0t, 1)

            def pair_products(m, c, first):
                w = pairs(c)
                if c == 0:
                    dve.wait_ge(s_rep, m + 1)
                if not (first and c < 2):
                    dve.wait_ge(s_l0, PAIR_CHUNKS * m + c - 1)
                dve.wait_ge(s_side, SIDE * m + 4 + c)
                nc.vector.tensor_tensor(quad[0:w, c % 2, :], side[0:w, (3 + c) % 2, :], x0_rep[0:w, :],
                                        ALU.mult).then_inc(s_quad, 1)

            def x1_split_lo(m, part):
                a, b = X1_PARTS[part]
                dve.wait_ge(s_x1h, 2 * m + part + 1)
                nc.vector.tensor_tensor(x1_lo[:, a:b], x1[:, a:b], x1_hi[:, a:b].bitcast(F32),
                                        ALU.subtract).then_inc(s_x1l, 1)

            def sum_x1(m):
                nc.vector.tensor_reduce(z1[:, bass.ds(m * BLOCK_B, BLOCK_B)],
                                        x1[:, :].rearrange("p (b d) -> p b d", d=D), AX_X,
                                        ALU.add).then_inc(s_z1, 1)

            def move_x0_t(n, first):
                dve.wait_ge(s_x0t, n + 1)
                if not first:
                    dve.wait_ge(s_mul, n * (TILES * MUL_TILE))
                    dve.wait_ge(s_stt, n * (TILES * STT_TILE))
                    dve.wait_ge(s_pool, n * POOL_BLOCK - POOL_BLOCK + TILES)
                nc.vector.tensor_copy(x0_t[:, :, 0:F], x0_t_next[:, :, :]).then_inc(s_cur, 1)

            def sums(n, g, first):
                t, c = divmod(g, CHUNKS)
                base = n * (TILES * STT_TILE) + t * STT_TILE
                k = sum(len(FIELDS[x]) for x in DVE_CHUNKS if x < c)
                if g == 0:
                    dve.wait_ge(s_cur, n + 1)
                if k == 0 and not (first and t < 2):
                    dve.wait_ge(s_pool, n * POOL_BLOCK + (pool_done(t - 2, POOL_TILE) if t >= 2 else
                                                          pool_done(TILES + t - 2, POOL_TILE) - POOL_BLOCK))
                dve.wait_ge(s_v, n * SLOTS + g + 1)
                for x, j in enumerate(FIELDS[c]):
                    into, term, weight = acc[:, t % 2, k % 2, :], v[:, g % VBANKS, x * H:(x + 1) * H], x0_t[:, t, j:j + 1]
                    if k >= 2:
                        dve.wait_ge(s_stt, base + k - 1)
                    if k == 1:
                        nc.vector.tensor_scalar(into, term, weight, None, ALU.mult).then_inc(s_stt, 1)
                    else:
                        nc.vector.scalar_tensor_tensor(out=into, in0=term, scalar=weight,
                                                       in1=b1_row[:, :] if k == 0 else into,
                                                       op0=ALU.mult, op1=ALU.add).then_inc(s_stt, 1)
                    k += 1
                if c == DVE_CHUNKS[-1]:
                    dve.wait_ge(s_stt, base + k)
                    nc.vector.tensor_tensor(acc[:, t % 2, 0, :], acc[:, t % 2, 0, :], acc[:, t % 2, 1, :],
                                            ALU.add).then_inc(s_stt, 1)

            def step(n, first=False, last=False):
                for g in range(SLOTS):
                    if g == 0:
                        if not first:
                            x1_split_lo(n, 1)
                        move_x0_t(n, first)
                    if not last:
                        m = n + 1
                        if g == S_SPLIT + 1:
                            split_lo(m)
                        if g == S_REPPED:
                            copy_x0_t(m, False)
                        c, off = divmod(g - S_QUAD, 3)
                        if off == 0 and 0 <= c < PAIR_CHUNKS:
                            pair_products(m, c, False)
                        if g == S_X1 + 1:
                            x1_split_lo(m, 0)
                            sum_x1(m)
                    if g % CHUNKS in DVE_CHUNKS:
                        sums(n, g, first)

            nc.vector.memset(emb_parts[:, :, F:LO].bitcast(F32), 0.0).then_inc(s_zeroed, 1)
            nc.vector.memset(x0_t[:, :, F:FE], 1.0).then_inc(s_zeroed, 1)
            dve.wait_ge(s_w0, 16)
            nc.vector.tensor_copy(w0_sym[:, 0, :], w0_raw[:, 0:F * F:F + 1])
            for delta in range(1, NDELTA):
                for j0, j1, wrap in ((0, F - delta, 0), (F - delta, F, F)):
                    a = j0 * (F + 1) + delta - wrap
                    b = j0 * (F + 1) + F * delta - F * wrap
                    last_row = (j1 - j0 - 1) * (F + 1) + 1
                    ins = nc.vector.tensor_tensor(w0_sym[:, delta, j0:j1], w0_raw[:, a:a + last_row:F + 1],
                                                  w0_raw[:, b:b + last_row:F + 1], ALU.add)
            ins.then_inc(s_sym, 1)
            for c in range(CHUNKS):
                a, w = c * JC * H, len(FIELDS[c]) * H
                dve.wait_ge(s_tr_hi, W1_GROUP0 + c + 1)
                nc.vector.tensor_tensor(w1_lo[:, a:a + w], v[:, (W1_GROUP0 + c) % VBANKS, 0:w],
                                        w1_hi[:, a:a + w].bitcast(F32), ALU.subtract).then_inc(s_tr_lo, 1)
            dve.wait_ge(s_bias, 16 * NBIAS)
            split_lo(0)
            copy_x0_t(0, True)
            for c in range(PAIR_CHUNKS):
                pair_products(0, c, True)
            for part in range(2):
                x1_split_lo(0, part)
            sum_x1(0)
            step(0, first=True)
            with dve.Fori(1, NBLOCKS - 1) as i:
                step(i)
            step(NBLOCKS - 1, last=True)

        @block.tensor
        def _(pe):
            def turn(m, first):
                pe.wait_ge(s_lo, m + 1)
                if not first:
                    pe.wait_ge(s_quad, PAIR_CHUNKS * m - 1)
                else:
                    pe.wait_ge(s_sel, 2)
                for d in range(D):
                    ins = nc.tensor.matmul(side[0:XROWS, 0, d * BLOCK_B:(d + 1) * BLOCK_B], emb_parts[:, d, :],
                                           ident_r[:, :], start=True, stop=True)
                ins.then_inc(s_side, 1)

            def replicate(m, first):
                pe.wait_ge(s_x0, m + 1)
                if first:
                    pe.wait_ge(s_sel, 1)
                else:
                    pe.wait_ge(s_quad, PAIR_CHUNKS * m)
                nc.tensor.matmul(side[0:PAIRS, 1, :], sel_rep, x0[:, :], start=True, stop=True).then_inc(s_side, 1)

            def turn_back(m):
                for t in range(TILES):
                    ins = nc.tensor.matmul(side[:, 0, t * FE:(t + 1) * FE], x0[:, t * P:(t + 1) * P], sel_fields,
                                           start=True, stop=True)
                ins.then_inc(s_side, 1)

            def pair_rows(m, c):
                if c == 0:
                    pe.wait_ge(s_rep, m + 1)
                elif c == 1:
                    pe.wait_ge(s_x0t, m + 1)
                else:
                    pe.wait_ge(s_quad, PAIR_CHUNKS * m + c - 1)
                nc.tensor.matmul(side[0:pairs(c), (3 + c) % 2, :], sel_pair(c), x0[:, :], start=True,
                                 stop=True).then_inc(s_side, 1)

            def layer0(m, c, first):
                if c == 0 and not first:
                    pe.wait_ge(s_x1, m)
                pe.wait_ge(s_quad, PAIR_CHUNKS * m + c + 1)
                nc.tensor.matmul(x1_ps[:, :], w0_t[0:pairs(c), c, :], quad[0:pairs(c), c % 2, :], start=(c == 0),
                                 stop=(c == PAIR_CHUNKS - 1)).then_inc(s_l0, 1)

            def layer1(n, g, first):
                t, c = divmod(g, CHUNKS)
                if c == 0 and t in (0, TILES - 1):
                    pe.wait_ge(s_x1l, 2 * n + 1 + (t > 0))
                if not (first and g < VBANKS):
                    was = g - VBANKS
                    back = was < 0
                    was += SLOTS * back
                    if was % CHUNKS in DVE_CHUNKS:
                        pe.wait_ge(s_stt, n * (TILES * STT_TILE) + stt_done(was) - back * TILES * STT_TILE)
                    else:
                        pe.wait_ge(s_mul, n * (TILES * MUL_TILE) + mul_done(was) - back * TILES * MUL_TILE)
                w = len(FIELDS[c]) * H
                a = c * JC * H
                hi, lo, out = x1_hi[:, t * P:(t + 1) * P], x1_lo[:, t * P:(t + 1) * P], v[:, g % VBANKS, 0:w]
                nc.tensor.matmul(out, hi, w1_hi[:, a:a + w], start=True, stop=False)
                nc.tensor.matmul(out, hi, w1_lo[:, a:a + w], start=False, stop=False)
                nc.tensor.matmul(out, lo, w1_hi[:, a:a + w], start=False, stop=True).then_inc(s_v, 1)

            def form_g2(n, t, first):
                if not (first and t == 0):
                    pe.wait_ge(s_g2e, n * TILES + t)
                pe.wait_ge(s_pool, n * POOL_BLOCK + pool_done(t, POOL_TILE))
                nc.tensor.matmul(g2_ps[:, 0:TILE_B * FE], x2_t[:, t % 2, :], spread[:, t, :], start=True,
                                 stop=True).then_inc(s_g2, 1)

            def step(n, first=False, last=False):
                for g in range(SLOTS):
                    layer1(n, g, first)
                    if not last:
                        m = n + 1
                        if g == S_TURN:
                            turn(m, False)
                        if g == S_REP:
                            replicate(m, False)
                            turn_back(m)
                        c, off = divmod(g - S_PAIR, 3)
                        if off == 0 and 0 <= c < PAIR_CHUNKS:
                            pair_rows(m, c)
                        c, off = divmod(g - S_L0, 3)
                        if off == 0 and 0 <= c < PAIR_CHUNKS:
                            layer0(m, c, False)
                    t, lag = divmod(g - LAG_G2, CHUNKS)
                    if lag == 0 and t >= 1:
                        form_g2(n, t - 1, first)
                    if lag == 0 and t == 0 and not first:
                        form_g2(n - 1, TILES - 1, False)

            pe.wait_ge(s_const, 48)
            for s in range(GROUPS):
                if s >= VBANKS:
                    pe.wait_ge(s_tr_hi, s - VBANKS + 1)
                    if s - VBANKS >= W1_GROUP0:
                        pe.wait_ge(s_tr_lo, min(s - VBANKS - W1_GROUP0 + 1, CHUNKS))
                bank = v[:, s % VBANKS, :]
                if s < 3:
                    if s == 0:
                        pe.wait_ge(s_sym, 1)
                    c0, c1 = [(0, 4), (4, 6), (6, 7)][s]
                    for c in range(c0, c1):
                        d0, d1 = PER_CHUNK * c, min(PER_CHUNK * c + PER_CHUNK, NDELTA)
                        ins = nc.tensor.transpose(bank[0:pairs(c), (c - c0) * H:(c - c0 + 1) * H],
                                                  w0_sym[:, d0:d1, :].rearrange("h e j -> h (e j)"), ident[:, :])
                elif s == 3:
                    pe.wait_ge(s_dense, 16)
                    for t in range(BTILES):
                        ins = nc.tensor.transpose(bank[0:D, t * P:(t + 1) * P], dense_raw[:, t, :], ident[:, :])
                else:
                    raw, c, loaded = (w1_raw, s - W1_GROUP0, s_w1) if s < W2_GROUP0 else (w2_raw, s - W2_GROUP0, s_w2)
                    pe.wait_ge(loaded, 16)
                    for x, j in enumerate(FIELDS[c]):
                        ins = nc.tensor.transpose(bank[:, x * H:(x + 1) * H], raw[:, j * H:(j + 1) * H], ident[:, :])
                ins.then_inc(s_tr, 1)
            turn(0, True)
            replicate(0, True)
            turn_back(0)
            for c in range(PAIR_CHUNKS):
                pair_rows(0, c)
                if c >= 1:
                    layer0(0, c - 1, True)
            layer0(0, PAIR_CHUNKS - 1, True)
            pe.wait_ge(s_tr_hi, GROUPS)
            pe.wait_ge(s_tr_lo, CHUNKS)
            step(0, first=True)
            with pe.Fori(1, NBLOCKS - 1) as i:
                step(i)
            step(NBLOCKS - 1, last=True)
            form_g2(NBLOCKS - 1, TILES - 1, False)
            pe.wait_ge(s_g2e, NBLOCKS * TILES)
            pe.wait_ge(s_mul, NBLOCKS * TILES * MUL_TILE)
            pe.wait_ge(s_stt, NBLOCKS * TILES * STT_TILE)
            for j in range(F):
                ins = nc.tensor.matmul(v[:, 0, :], w2_t[:, j * H:(j + 1) * H], g2[:, j, :], start=(j == 0),
                                       stop=(j == F - 1))
            ins.then_inc(s_z3, 1)
            pe.wait_ge(s_top, 48)
            pe.wait_ge(s_z1, NBLOCKS)
            for c in range(4):
                cols = slice(c * P, (c + 1) * P)
                if c >= 2:
                    pe.wait_ge(s_m1e, c - 1)
                out = side[:, c % 2, :]
                nc.tensor.matmul(out, wt1_dense[:, cols], dense_t[:, :], start=True, stop=False)
                nc.tensor.matmul(out, wt1[:, 0, cols], z1[:, :], start=False, stop=False)
                nc.tensor.matmul(out, wt1[:, 1, cols], g2[:, F, :], start=False, stop=False)
                if c == 0:
                    pe.wait_ge(s_z3e, 1)
                nc.tensor.matmul(out, wt1[:, 2, cols], z3[:, :], start=False, stop=True).then_inc(s_m1, 1)
            for c in range(2):
                for k in range(4):
                    if c == 0:
                        pe.wait_ge(s_m1e, k + 1)
                    ins = nc.tensor.matmul(v[:, 1 + c, :], wt2[:, k, c * P:(c + 1) * P], h1[:, k, :], start=(k == 0),
                                           stop=(k == 3))
                ins.then_inc(s_m2, 1)
            for k in range(2):
                pe.wait_ge(s_m2e, k + 1)
                ins = nc.tensor.matmul(x1_ps[0:1, :], wt3[:, k:k + 1], h2[:, k, :], start=(k == 0), stop=(k == 1))
            ins.then_inc(s_y, 1)


def constants():
    ident = np.eye(P, dtype=np.float32)
    sel = np.zeros((XROWS, (PAIR_CHUNKS + 1) * PAIRS + FE), np.float32)
    for part in (0, LO):
        for r in range(PER_CHUNK):
            for j in range(F):
                sel[part + j, r * F + j] = 1.0
                for c in range(PAIR_CHUNKS):
                    if PER_CHUNK * c + r < NDELTA:
                        sel[part + (j + PER_CHUNK * c + r) % F, (1 + c) * PAIRS + r * F + j] = 1.0
        for j in range(F):
            sel[part + j, (PAIR_CHUNKS + 1) * PAIRS + j] = 1.0
    mask = np.zeros((P, TILE_B), np.float32)
    for p in range(P):
        mask[p, p // D] = 1.0
    return ident, sel, mask


def kernel(**inputs):
    import concourse.bacc as bacc
    from concourse.bass_utils import run_bass_kernel_spmd as run

    nc = bacc.Bacc("TRN2", target_bir_lowering=False, num_devices=1)
    arrays = {}

    def given(name, a):
        a = np.ascontiguousarray(a)
        arrays[f"in_{name}_dram"] = a
        return nc.dram_tensor(f"in_{name}_dram", a.shape, mybir.dt.from_np(a.dtype), kind="ExternalInput").ap()

    ids = given("ids", inputs["ids"])
    tables = [given(f"tbl_{j}", inputs[f"tbl_{j}"]) for j in range(F)]
    rest = [given(k, inputs[k]) for k in ("dense_ctx", "W_top1", "b_top1", "W_top2", "b_top2", "W_top3",
                                          "L0_rec_W0", "L0_rec_b0", "L0_rec_W1", "L0_rec_b1",
                                          "L0_rec_W2", "L0_rec_b2")]
    fixed = [given(k, a) for k, a in zip(("ident", "sel", "mask"), constants())]
    y = nc.dram_tensor("out_y_dram", (B, 1), F32, kind="ExternalOutput").ap()
    bass_dlrm(nc, ids, tables, *rest, *fixed, y)
    r = run(nc, [arrays], core_ids=[0])
    return r.results[0]["out_y_dram"]
```

```python
from contextlib import ExitStack

import numpy as np
import concourse.bass as bass
from concourse import mybir

ALU = mybir.AluOpType
ACT = mybir.ActivationFunctionType
AX_X = mybir.AxisListType.X
F32 = mybir.dt.float32
F32R = mybir.dt.float32r
I32 = mybir.dt.int32

P = 128
B, F, D = 512, 39, 16
H = 128
NDELTA = (F + 1) // 2
PER_CHUNK = 3
PAIR_CHUNKS = -(-NDELTA // PER_CHUNK)
PAIRS = PER_CHUNK * F
XROWS = 2 * F
BLOCK_B = 32
NBLOCKS = B // BLOCK_B
COLS = BLOCK_B * D
TILE_B = P // D
TILES = COLS // P
BTILES = B // P
FE = F + 1
JC = 4
CHUNKS = -(-F // JC)
SLOTS = TILES * CHUNKS
VBANKS = 5
FIELDS = [list(range(c * JC, min(c * JC + JC, F))) for c in range(CHUNKS)]

ACT_CHUNKS = [1, 3, 5, 7, 9]
DVE_CHUNKS = [c for c in range(CHUNKS) if c not in ACT_CHUNKS]
STT_TILE = sum(len(FIELDS[c]) for c in DVE_CHUNKS) + 1
MUL_TILE = sum(len(FIELDS[c]) for c in ACT_CHUNKS)
NPROD = len(ACT_CHUNKS)
SUMS = NPROD - 2
POOL_TILE = 1 + SUMS + 1
POOL_BLOCK = TILES * POOL_TILE
X2_TILE = 2
SIDE = 2

S_TURN, S_TURNED, S_BACK, S_BACKED = 1, 2, 4, 5
S_QUAD, S_L0 = 9, 13
S_X1 = 32
FOLD = 6
LAG_X2, LAG_G2, LAG_G2E = 6, 9, 10
X1_PARTS = [(0, COLS - P), (COLS - P, COLS)]

NBIAS = 11
GATHERED_FIRST = F + 15


def bass_dlrm(nc, ids, tables, dense, w_top1, b_top1, w_top2, b_top2, w_top3,
              w0, b0, w1, b1, w2, b2, ident_c, mask_c, y):
    ctx = ExitStack()
    with ctx:
        def sb(name, shape, dt=F32, stack=ctx):
            return stack.enter_context(nc.sbuf_tensor(name, shape, dt))

        def sem(name):
            return ctx.enter_context(nc.semaphore(name))

        early = ExitStack()
        w0_raw = sb("w0_raw", [P, F * F], F32, early)
        w0_sym = sb("w0_sym", [P, NDELTA, F], F32, early)
        w1_raw = sb("w1_raw", [P, F * H], F32, early)
        w2_raw = sb("w2_raw", [P, F * H], F32, early)
        early.close()
        g2 = sb("g2", [P, FE, B])

        middle = ExitStack()
        w1_hi = sb("w1_hi", [P, F * H], F32R, middle)
        w1_lo = sb("w1_lo", [P, F * H], F32R, middle)
        middle.close()
        late = ExitStack()
        wt1 = sb("wt1", [P, 3, 512], F32, late)
        wt1_dense = sb("wt1_dense", [D, 512], F32, late)
        wt2 = sb("wt2", [P, 4, 256], F32, late)
        h1 = sb("h1", [P, 4, B], F32, late)
        h2 = sb("h2", [P, 2, B], F32, late)
        z3 = sb("z3", [P, B], F32, late)
        y_row = sb("y_row", [1, B], F32, late)
        dense_raw = sb("dense_raw", [P, BTILES, D], F32, late)
        dense_t = sb("dense_t", [D, B], F32, late)
        late.close()
        sb("w1_place", [P, 2 * F * H])

        ids_sb = sb("ids_sb", [P, BTILES, F], I32)
        emb = sb("emb", [P, BTILES, F * D])
        emb_block = sb("emb_block", [P, 2, F * D])
        ident = sb("ident", [P, P])
        mask = sb("mask", [P, TILE_B])
        w0_t = sb("w0_t", [PAIRS, PAIR_CHUNKS, H])
        w2_t = sb("w2_t", [P, F * H])
        x0 = sb("x0", [XROWS, COLS])
        x0_rep = sb("x0_rep", [PAIRS, COLS])
        quad = sb("quad", [PAIRS, PAIR_CHUNKS, COLS])
        x0_t_next = sb("x0_t_next", [P, TILES, F])
        x0_t = sb("x0_t", [P, TILES, FE])
        x1 = sb("x1", [P, COLS])
        x1_hi = sb("x1_hi", [P, COLS], F32R)
        x1_lo = sb("x1_lo", [P, COLS], F32R)
        acc = sb("acc", [P, 2, 2, H])
        prod = sb("prod", [P, NPROD, JC * H])
        partial = sb("partial", [P, JC * H])
        x2_t = sb("x2_t", [P, 2, H])
        spread = sb("spread", [P, TILES, TILE_B * FE])
        b0_sb = sb("b0_sb", [P, 1])
        b1_row = sb("b1_row", [P, H])
        b2_sb = sb("b2_sb", [P, 1])
        b2_x16 = sb("b2_x16", [P, 1])
        bt1_sb = sb("bt1_sb", [P, 4])
        bt2_sb = sb("bt2_sb", [P, 2])
        wt3 = sb("wt3", [P, 2])
        z1 = sb("z1", [P, B])

        v = ctx.enter_context(nc.psum_tensor("v", [P, VBANKS, 512], F32))
        side = ctx.enter_context(nc.psum_tensor("side", [P, 512], F32))
        x1_ps = ctx.enter_context(nc.psum_tensor("x1_ps", [P, COLS], F32))
        g2_ps = ctx.enter_context(nc.psum_tensor("g2_ps", [P, 512], F32))

        def pairs(c):
            return min(PER_CHUNK, NDELTA - PER_CHUNK * c) * F

        s_ids, s_w0, s_w1, s_w2 = sem("s_ids"), sem("s_w0"), sem("s_w1"), sem("s_w2")
        s_const, s_bias, s_dense = sem("s_const"), sem("s_bias"), sem("s_dense")
        s_gathered = sem("s_gathered")
        s_block = sem("s_block")
        s_top = sem("s_top")
        s_out = sem("s_out")
        s_zeroed = sem("s_zeroed")
        s_sym = sem("s_sym")
        s_tr = sem("s_tr")
        s_tr_hi = sem("s_tr_hi")
        s_tr_lo = sem("s_tr_lo")
        s_scaled = sem("s_scaled")
        s_side = sem("s_side")
        s_x0 = sem("s_x0")
        s_rep = sem("s_rep")
        s_pair = [sem(f"s_pair{c}") for c in range(PAIR_CHUNKS)]
        s_x0t = sem("s_x0t")
        s_quad = sem("s_quad")
        s_l0 = sem("s_l0")
        s_x1 = sem("s_x1")
        s_x1h = sem("s_x1h")
        s_x1l = sem("s_x1l")
        s_z1 = sem("s_z1")
        s_cur = sem("s_cur")
        s_v = sem("s_v")
        s_stt = sem("s_stt")
        s_mul = sem("s_mul")
        s_pool = sem("s_pool")
        s_fold = sem("s_fold")
        s_x2 = sem("s_x2")
        s_dense_t = sem("s_dense_t")
        s_g2 = sem("s_g2")
        s_g2e = sem("s_g2e")
        s_z3 = sem("s_z3")
        s_z3e = sem("s_z3e")
        s_m1, s_m1e = sem("s_m1"), sem("s_m1e")
        s_m2, s_m2e = sem("s_m2"), sem("s_m2e")
        s_y, s_ye = sem("s_y"), sem("s_ye")

        W1_GROUP0 = 3
        W2_GROUP0 = W1_GROUP0 + CHUNKS
        GROUPS = W2_GROUP0 + CHUNKS

        def stt_done(g):
            t, c = divmod(g, CHUNKS)
            return STT_TILE * t + sum(len(FIELDS[x]) for x in DVE_CHUNKS if x <= c)

        def mul_done(g):
            t, c = divmod(g, CHUNKS)
            return MUL_TILE * t + sum(len(FIELDS[x]) for x in ACT_CHUNKS if x <= c)

        def late(n, g, lag, first):
            t, off = divmod(g - lag, CHUNKS)
            if off or (first and t < 1):
                return []
            return [(n, t - 1)] if t >= 1 else [(n - 1, t - 1 + TILES)]

        def left(lag):
            return [(NBLOCKS - 1, t) for t in range(TILES) if CHUNKS * (t + 1) + lag >= SLOTS]

        def pool_done(t, step):
            return POOL_TILE * t + 1 + step

        block = ctx.enter_context(nc.Block())

        @block.sync
        def _(sp):
            sp.dma_start(ids_sb[:, :, :], ids.rearrange("(t p) f -> p t f", p=P)).then_inc(s_ids, 16)
            sp.dma_start(w0_raw[:, :], w0).then_inc(s_w0, 16)
            sp.dma_start(ident[:, :], ident_c).then_inc(s_const, 16)
            sp.dma_start(mask[:, :], mask_c).then_inc(s_const, 16)
            sp.dma_start(w1_raw[:, :], w1).then_inc(s_w1, 16)
            sp.dma_start(b0_sb[:, :], b0.rearrange("(h o) -> h o", o=1)).then_inc(s_bias, 16)
            sp.dma_start(b2_sb[:, :], b2.rearrange("(h o) -> h o", o=1)).then_inc(s_bias, 16)
            sp.dma_start(b1_row[:, :], b1.rearrange("(o h) -> o h", o=1).broadcast_to([P, H])).then_inc(s_bias, 16)
            for c in range(4):
                sp.dma_start(bt1_sb[:, c:c + 1], b_top1[c * P:(c + 1) * P].rearrange("(h o) -> h o", o=1)).then_inc(s_bias, 16)
            for c in range(2):
                sp.dma_start(bt2_sb[:, c:c + 1], b_top2[c * P:(c + 1) * P].rearrange("(h o) -> h o", o=1)).then_inc(s_bias, 16)
                sp.dma_start(wt3[:, c:c + 1], w_top3[c * P:(c + 1) * P, :]).then_inc(s_bias, 16)
            sp.dma_start(w2_raw[:, :], w2).then_inc(s_w2, 16)

            def stage(t, q):
                m = t * (P // BLOCK_B) + q
                if q == 0:
                    sp.wait_ge(s_gathered, t * (16 * F) + 16 * F)
                for half in range(2):
                    sp.dma_start(emb_block[0:BLOCK_B, half, :],
                                 emb[q * BLOCK_B:(q + 1) * BLOCK_B, t, :]).then_inc(s_block, 16)
                sp.wait_ge(s_x0, m + 1)
                for r in range(PER_CHUNK):
                    sp.dma_start(x0_rep[r * F:(r + 1) * F, :], x0[0:F, :]).then_inc(s_rep, 16)
                for c in range(PAIR_CHUNKS):
                    for r in range(pairs(c) // F):
                        delta = PER_CHUNK * c + r
                        sp.dma_start(quad[r * F:(r + 1) * F, c, :], x0[delta:delta + F, :]).then_inc(s_pair[c], 16)

            sp.wait_ge(s_zeroed, 1)
            with sp.Fori(0, BTILES) as t:
                for q in range(P // BLOCK_B):
                    stage(t, q)
            sp.wait_ge(s_v, SLOTS * NBLOCKS)
            sp.dma_start(wt1[:, :, :], w_top1[0:3 * P, :].rearrange("(c p) m -> p c m", p=P)).then_inc(s_top, 16)
            sp.dma_start(wt1_dense[:, :], w_top1[3 * P:3 * P + D, :]).then_inc(s_top, 16)
            sp.dma_start(dense_raw[:, :, :], dense.rearrange("(t p) f -> p t f", p=P)).then_inc(s_dense, 16)
            sp.dma_start(wt2[:, :, :], w_top2.rearrange("(c p) m -> p c m", p=P)).then_inc(s_top, 16)
            sp.wait_ge(s_ye, 1)
            sp.dma_start(y.rearrange("b o -> o b"), y_row[:, :]).then_inc(s_out, 16)
            sp.wait_ge(s_out, 16)

        @block.gpsimd
        def _(pool):
            order = [(t, j) for t in range(BTILES) for j in range(F)]

            def gather(n):
                for t, j in order[:n]:
                    if j == 0 and t > 0:
                        pool.wait_ge(s_gathered, 16 * F * t)
                    nc.gpsimd.indirect_dma_start(
                        emb[:, t, j * D:(j + 1) * D], None, tables[j],
                        bass.IndirectOffsetOnAxis(ids_sb[:, t, j:j + 1], 0)).then_inc(s_gathered, 16)
                del order[:n]

            def x1_split_lo(m, part):
                a, b = X1_PARTS[part]
                pool.wait_ge(s_x1h, 2 * m + part + 1)
                nc.gpsimd.tensor_tensor(x1_lo[:, a:b], x1[:, a:b], x1_hi[:, a:b].bitcast(F32),
                                        ALU.subtract).then_inc(s_x1l, 1)

            def spread_x0(n, t, first):
                if t == 0:
                    pool.wait_ge(s_cur, n + 1)
                if not first:
                    pool.wait_ge(s_g2, n * TILES + t + 1 - TILES)
                nc.gpsimd.tensor_tensor(
                    spread[:, t, :].rearrange("p (b j) -> p b j", b=TILE_B),
                    mask[:, :].unsqueeze(2).broadcast_to([P, TILE_B, FE]),
                    x0_t[:, t, :].unsqueeze(1).broadcast_to([P, TILE_B, FE]), ALU.mult).then_inc(s_pool, 1)

            def sum_tile(n, t):
                base, muls = n * POOL_BLOCK, n * (TILES * MUL_TILE)
                for k in range(1, SUMS + 1):
                    w = len(FIELDS[ACT_CHUNKS[k + 1]]) * H
                    pool.wait_ge(s_pool, base + pool_done(t, k - 1))
                    if k == 1:
                        if not (isinstance(n, int) and n == 0 and t == 0):
                            pool.wait_ge(s_x2, (n * TILES + t) * X2_TILE)
                        pool.wait_ge(s_fold, n * TILES + t + 1)
                    pool.wait_ge(s_mul, muls + mul_done(t * CHUNKS + ACT_CHUNKS[k + 1]))
                    nc.gpsimd.tensor_tensor(partial[:, 0:w], prod[:, 0, :] if k == 1 else partial[:, 0:w],
                                            prod[:, k + 1, 0:w], ALU.add).then_inc(s_pool, 1)
                pool.wait_ge(s_pool, base + pool_done(t, SUMS))
                nc.gpsimd.tensor_tensor(partial[:, 0:2 * H], partial[:, 0:2 * H], partial[:, 2 * H:4 * H],
                                        ALU.add).then_inc(s_pool, 1)

            pool.wait_ge(s_ids, 16)
            gather(GATHERED_FIRST)
            pool.wait_ge(s_const, 32)

            def step(n, first=False, last=False, gathers=0):
                for t in range(TILES):
                    spread_x0(n, t, first)
                    if t == 1 and not first:
                        x1_split_lo(n, 1)
                    if t == TILES - 1 and not last:
                        x1_split_lo(n + 1, 0)
                    sum_tile(n, t)
                    gather(gathers + t % 2 if gathers else 0)

            for part in range(2):
                x1_split_lo(0, part)
            n = 0
            while order:
                step(n, first=(n == 0), gathers=2)
                n += 1
            with pool.Fori(n, NBLOCKS - 1) as i:
                step(i)
            step(NBLOCKS - 1, last=True)

        @block.scalar
        def _(act):
            def copy_x0(m, first):
                act.wait_ge(s_side, m * SIDE + 1)
                if not first:
                    act.wait_ge(s_l0, m * PAIR_CHUNKS)
                nc.scalar.activation(x0[:, :].rearrange("p (b d) -> p d b", d=D),
                                     side[0:XROWS, :].rearrange("p (d b) -> p d b", d=D),
                                     ACT.Copy).then_inc(s_x0, 1)

            def copy_x0_t(m, first):
                act.wait_ge(s_side, m * SIDE + 2)
                if not first:
                    act.wait_ge(s_cur, m)
                nc.scalar.activation(x0_t_next[:, :, :],
                                     side[:, 0:TILES * XROWS].rearrange("p (t j) -> p t j", j=XROWS)[:, :, 0:F],
                                     ACT.Copy).then_inc(s_x0t, 1)

            def move_x0_t(n, first):
                act.wait_ge(s_x0t, n + 1)
                if first:
                    act.wait_ge(s_zeroed, 2)
                else:
                    act.wait_ge(s_mul, n * (TILES * MUL_TILE))
                    act.wait_ge(s_stt, n * (TILES * STT_TILE))
                    act.wait_ge(s_pool, n * POOL_BLOCK + pool_done(TILES - 1, 0) - POOL_BLOCK)
                nc.scalar.activation(x0_t[:, :, 0:F], x0_t_next[:, :, :], ACT.Copy).then_inc(s_cur, 1)

            def copy_x1(m, first):
                act.wait_ge(s_l0, PAIR_CHUNKS * (m + 1))
                if not first:
                    act.wait_ge(s_x1l, 2 * m)
                    act.wait_ge(s_z1, m)
                nc.scalar.activation(x1[:, :], x1_ps[:, :], ACT.Identity, bias=b0_sb[:, 0:1]).then_inc(s_x1, 1)

            def x1_split_hi(m, part, first):
                a, b = X1_PARTS[part]
                act.wait_ge(s_x1, m + 1)
                if not first:
                    act.wait_ge(s_v, SLOTS * m - SLOTS + CHUNKS * (b // P))
                nc.scalar.activation(x1_hi[:, a:b], x1[:, a:b], ACT.Copy).then_inc(s_x1h, 1)

            def products(n, g, first):
                t, c = divmod(g, CHUNKS)
                k = ACT_CHUNKS.index(c)
                if g == ACT_CHUNKS[0]:
                    act.wait_ge(s_cur, n + 1)
                if not (first and t == 0):
                    if k == 1:
                        act.wait_ge(s_fold, n * TILES + t)
                    else:
                        act.wait_ge(s_pool, n * POOL_BLOCK + pool_done(t - 1, max(k - 1, 1)))
                act.wait_ge(s_v, n * SLOTS + g + 1)
                for x, j in enumerate(FIELDS[c]):
                    nc.scalar.activation(prod[:, k, x * H:(x + 1) * H], v[:, g % VBANKS, x * H:(x + 1) * H],
                                         ACT.Copy, scale=x0_t[:, t, j:j + 1]).then_inc(s_mul, 1)

            def copy_g2(n, t):
                b_at = n * BLOCK_B + t * TILE_B
                act.wait_ge(s_g2, n * TILES + t + 1)
                act.wait_ge(s_tr_hi, GROUPS)
                nc.scalar.activation(g2[:, :, bass.ds(b_at, TILE_B)],
                                     g2_ps[:, 0:TILE_B * FE].rearrange("p (b j) -> p j b", b=TILE_B),
                                     ACT.Copy).then_inc(s_g2e, 1)

            def step(n, first=False, last=False):
                for g in range(SLOTS):
                    if g == 0:
                        move_x0_t(n, first)
                        if not first:
                            x1_split_hi(n, 1, False)
                    if not last:
                        m = n + 1
                        if g == S_BACKED:
                            copy_x0_t(m, False)
                        if g == S_TURNED:
                            copy_x0(m, False)
                        if g == S_X1:
                            copy_x1(m, False)
                            x1_split_hi(m, 0, False)
                    for at in late(n, g, LAG_G2E, first):
                        copy_g2(*at)
                    if g % CHUNKS in ACT_CHUNKS:
                        products(n, g, first)

            for s in range(GROUPS):
                act.wait_ge(s_tr, s + 1)
                bank = v[:, s % VBANKS, :]
                if s < 3:
                    rows, c0, c1 = [(PAIRS, 0, 4), (PAIRS, 4, 6), (pairs(6), 6, 7)][s]
                    nc.scalar.activation(w0_t[0:rows, c0:c1, :].rearrange("p c h -> p (c h)"),
                                         bank[0:rows, 0:(c1 - c0) * H], ACT.Copy).then_inc(s_tr_hi, 1)
                else:
                    dst, c = (w1_hi, s - W1_GROUP0) if s < W2_GROUP0 else (w2_t, s - W2_GROUP0)
                    w = len(FIELDS[c]) * H
                    nc.scalar.activation(dst[:, c * JC * H:c * JC * H + w], bank[:, 0:w], ACT.Copy).then_inc(s_tr_hi, 1)
            act.wait_ge(s_bias, 16 * NBIAS)
            nc.scalar.mul(b2_x16[:, :], b2_sb[:, :], float(D)).then_inc(s_scaled, 1)
            copy_x0(0, True)
            copy_x0_t(0, True)
            copy_x1(0, True)
            for part in range(2):
                x1_split_hi(0, part, True)
            step(0, first=True)
            with act.Fori(1, NBLOCKS - 1) as i:
                step(i)
            step(NBLOCKS - 1, last=True)
            for at in left(LAG_G2E):
                copy_g2(*at)
            act.wait_ge(s_dense_t, 1)
            nc.scalar.activation(dense_t[:, :], side[0:D, :], ACT.Copy).then_inc(s_dense_t, 1)
            act.wait_ge(s_scaled, 1)
            act.wait_ge(s_z3, 1)
            nc.scalar.activation(z3[:, :], v[:, 0, :], ACT.Identity, bias=b2_x16[:, 0:1]).then_inc(s_z3e, 1)
            for c in range(4):
                act.wait_ge(s_m1, c + 1)
                nc.scalar.activation(h1[:, c, :], v[:, 3 + c % 2, :], ACT.Relu, bias=bt1_sb[:, c:c + 1]).then_inc(s_m1e, 1)
            for c in range(2):
                act.wait_ge(s_m2, c + 1)
                nc.scalar.activation(h2[:, c, :], v[:, 1 + c, :], ACT.Relu, bias=bt2_sb[:, c:c + 1]).then_inc(s_m2e, 1)
            act.wait_ge(s_y, 1)
            nc.scalar.activation(y_row[:, :], x1_ps[0:1, :], ACT.Copy).then_inc(s_ye, 1)

        @block.vector
        def _(dve):
            def pair_products(m, c):
                w = pairs(c)
                if c == 0:
                    dve.wait_ge(s_rep, m * (16 * PER_CHUNK) + 16 * PER_CHUNK)
                dve.wait_ge(s_pair[c], m * (16 * w // F) + 16 * w // F)
                nc.vector.tensor_tensor(quad[0:w, c, :], quad[0:w, c, :], x0_rep[0:w, :], ALU.mult).then_inc(s_quad, 1)

            def sum_x1(m):
                dve.wait_ge(s_x1, m + 1)
                nc.vector.tensor_reduce(z1[:, bass.ds(m * BLOCK_B, BLOCK_B)],
                                        x1[:, :].rearrange("p (b d) -> p b d", d=D), AX_X,
                                        ALU.add).then_inc(s_z1, 1)

            def sums(n, g, first):
                t, c = divmod(g, CHUNKS)
                base = n * (TILES * STT_TILE) + t * STT_TILE
                k = sum(len(FIELDS[x]) for x in DVE_CHUNKS if x < c)
                if g == 0:
                    dve.wait_ge(s_cur, n + 1)
                if k == 0 and not (first and t < 2):
                    dve.wait_ge(s_x2, (n * TILES + t - 1) * X2_TILE)
                dve.wait_ge(s_v, n * SLOTS + g + 1)
                for x, j in enumerate(FIELDS[c]):
                    into, term, weight = acc[:, t % 2, k % 2, :], v[:, g % VBANKS, x * H:(x + 1) * H], x0_t[:, t, j:j + 1]
                    if k >= 2:
                        dve.wait_ge(s_stt, base + k - 1)
                    if k == 1:
                        nc.vector.tensor_scalar(into, term, weight, None, ALU.mult).then_inc(s_stt, 1)
                    else:
                        nc.vector.scalar_tensor_tensor(out=into, in0=term, scalar=weight,
                                                       in1=b1_row[:, :] if k == 0 else into,
                                                       op0=ALU.mult, op1=ALU.add).then_inc(s_stt, 1)
                    k += 1
                if c == DVE_CHUNKS[-1]:
                    dve.wait_ge(s_stt, base + k)
                    nc.vector.tensor_tensor(acc[:, t % 2, 0, :], acc[:, t % 2, 0, :], acc[:, t % 2, 1, :],
                                            ALU.add).then_inc(s_stt, 1)

            def fold(n, t):
                dve.wait_ge(s_mul, n * (TILES * MUL_TILE) + mul_done(t * CHUNKS + ACT_CHUNKS[1]))
                nc.vector.tensor_tensor(prod[:, 0, :], prod[:, 0, :], prod[:, 1, :], ALU.add).then_inc(s_fold, 1)

            def finish_x2(n, t):
                slot = t % 2
                dve.wait_ge(s_stt, (n * TILES + t + 1) * STT_TILE)
                dve.wait_ge(s_pool, n * POOL_BLOCK + pool_done(t, SUMS + 1))
                nc.vector.tensor_tensor(acc[:, slot, 0, :], acc[:, slot, 0, :], partial[:, 0:H],
                                        ALU.add).then_inc(s_x2, 1)
                dve.wait_ge(s_x2, (n * TILES + t) * X2_TILE + 1)
                if not (isinstance(n, int) and n == 0 and t < 2):
                    dve.wait_ge(s_g2, n * TILES + t - 1)
                nc.vector.tensor_tensor(x2_t[:, slot, :], acc[:, slot, 0, :], partial[:, H:2 * H],
                                        ALU.add).then_inc(s_x2, 1)

            def step(n, first=False, last=False):
                for g in range(SLOTS):
                    if not last:
                        m = n + 1
                        c, off = divmod(g - S_QUAD, 3)
                        if off == 0 and 0 <= c < PAIR_CHUNKS:
                            pair_products(m, c)
                        if g == S_X1 + 1:
                            sum_x1(m)
                    if g % CHUNKS == FOLD:
                        fold(n, g // CHUNKS)
                    for at in late(n, g, LAG_X2, first):
                        finish_x2(*at)
                    if g % CHUNKS in DVE_CHUNKS:
                        sums(n, g, first)

            nc.vector.memset(emb_block[:, :, :], 0.0).then_inc(s_zeroed, 1)
            nc.vector.memset(x0_t[:, :, F:FE], 1.0).then_inc(s_zeroed, 1)
            dve.wait_ge(s_w0, 16)
            nc.vector.tensor_copy(w0_sym[:, 0, :], w0_raw[:, 0:F * F:F + 1])
            for delta in range(1, NDELTA):
                for j0, j1, wrap in ((0, F - delta, 0), (F - delta, F, F)):
                    a = j0 * (F + 1) + delta - wrap
                    b = j0 * (F + 1) + F * delta - F * wrap
                    last_row = (j1 - j0 - 1) * (F + 1) + 1
                    ins = nc.vector.tensor_tensor(w0_sym[:, delta, j0:j1], w0_raw[:, a:a + last_row:F + 1],
                                                  w0_raw[:, b:b + last_row:F + 1], ALU.add)
            ins.then_inc(s_sym, 1)
            for c in range(CHUNKS):
                a, w = c * JC * H, len(FIELDS[c]) * H
                dve.wait_ge(s_tr_hi, W1_GROUP0 + c + 1)
                nc.vector.tensor_tensor(w1_lo[:, a:a + w], v[:, (W1_GROUP0 + c) % VBANKS, 0:w],
                                        w1_hi[:, a:a + w].bitcast(F32), ALU.subtract).then_inc(s_tr_lo, 1)
            dve.wait_ge(s_bias, 16 * NBIAS)
            for c in range(PAIR_CHUNKS):
                pair_products(0, c)
            sum_x1(0)
            step(0, first=True)
            with dve.Fori(1, NBLOCKS - 1) as i:
                step(i)
            step(NBLOCKS - 1, last=True)
            for at in left(LAG_X2):
                finish_x2(*at)

        @block.tensor
        def _(pe):
            def turn(m, first):
                if not first:
                    pe.wait_ge(s_x0t, m)
                pe.wait_ge(s_block, m * 32 + 32)
                for d in range(D):
                    w = P if d == 0 else BLOCK_B
                    ins = nc.tensor.transpose(
                        side[0:XROWS, d * BLOCK_B:d * BLOCK_B + w],
                        emb_block[0:w, :, :].rearrange("b e (j d) -> b (e j) d", d=D)[:, :, d], ident[0:w, 0:w])
                ins.then_inc(s_side, 1)

            def turn_back(m):
                pe.wait_ge(s_x0, m + 1)
                for t in range(TILES):
                    ins = nc.tensor.transpose(side[:, t * XROWS:(t + 1) * XROWS], x0[:, t * P:(t + 1) * P],
                                              ident[0:XROWS, 0:XROWS])
                ins.then_inc(s_side, 1)

            def layer0(m, c, first):
                if c == 0 and not first:
                    pe.wait_ge(s_x1, m)
                pe.wait_ge(s_quad, PAIR_CHUNKS * m + c + 1)
                nc.tensor.matmul(x1_ps[:, :], w0_t[0:pairs(c), c, :], quad[0:pairs(c), c, :], start=(c == 0),
                                 stop=(c == PAIR_CHUNKS - 1)).then_inc(s_l0, 1)

            def layer1(n, g, first):
                t, c = divmod(g, CHUNKS)
                if c == 0 and t in (0, TILES - 1):
                    pe.wait_ge(s_x1l, 2 * n + 1 + (t > 0))
                if not (first and g < VBANKS):
                    was = g - VBANKS
                    back = was < 0
                    was += SLOTS * back
                    if was % CHUNKS in DVE_CHUNKS:
                        pe.wait_ge(s_stt, n * (TILES * STT_TILE) + stt_done(was) - back * TILES * STT_TILE)
                    else:
                        pe.wait_ge(s_mul, n * (TILES * MUL_TILE) + mul_done(was) - back * TILES * MUL_TILE)
                w = len(FIELDS[c]) * H
                a = c * JC * H
                hi, lo, out = x1_hi[:, t * P:(t + 1) * P], x1_lo[:, t * P:(t + 1) * P], v[:, g % VBANKS, 0:w]
                nc.tensor.matmul(out, hi, w1_hi[:, a:a + w], start=True, stop=False)
                nc.tensor.matmul(out, hi, w1_lo[:, a:a + w], start=False, stop=False)
                nc.tensor.matmul(out, lo, w1_hi[:, a:a + w], start=False, stop=True).then_inc(s_v, 1)

            def form_g2(n, t):
                if not (isinstance(n, int) and n == 0 and t == 0):
                    pe.wait_ge(s_g2e, n * TILES + t)
                pe.wait_ge(s_x2, (n * TILES + t + 1) * X2_TILE)
                nc.tensor.matmul(g2_ps[:, 0:TILE_B * FE], x2_t[:, t % 2, :], spread[:, t, :], start=True,
                                 stop=True).then_inc(s_g2, 1)

            def step(n, first=False, last=False):
                for g in range(SLOTS):
                    layer1(n, g, first)
                    if not last:
                        m = n + 1
                        if g == S_TURN:
                            turn(m, False)
                        if g == S_BACK:
                            turn_back(m)
                        c, off = divmod(g - S_L0, 3)
                        if off == 0 and 0 <= c < PAIR_CHUNKS:
                            layer0(m, c, False)
                    for at in late(n, g, LAG_G2, first):
                        form_g2(*at)

            pe.wait_ge(s_const, 32)
            for s in range(GROUPS):
                if s >= VBANKS:
                    pe.wait_ge(s_tr_hi, s - VBANKS + 1)
                    if s - VBANKS >= W1_GROUP0:
                        pe.wait_ge(s_tr_lo, min(s - VBANKS - W1_GROUP0 + 1, CHUNKS))
                bank = v[:, s % VBANKS, :]
                if s < 3:
                    if s == 0:
                        pe.wait_ge(s_sym, 1)
                    c0, c1 = [(0, 4), (4, 6), (6, 7)][s]
                    for c in range(c0, c1):
                        d0, d1 = PER_CHUNK * c, min(PER_CHUNK * c + PER_CHUNK, NDELTA)
                        ins = nc.tensor.transpose(bank[0:pairs(c), (c - c0) * H:(c - c0 + 1) * H],
                                                  w0_sym[:, d0:d1, :].rearrange("h e j -> h (e j)"), ident[:, :])
                else:
                    raw, c, loaded = (w1_raw, s - W1_GROUP0, s_w1) if s < W2_GROUP0 else (w2_raw, s - W2_GROUP0, s_w2)
                    pe.wait_ge(loaded, 16)
                    for x, j in enumerate(FIELDS[c]):
                        ins = nc.tensor.transpose(bank[:, x * H:(x + 1) * H], raw[:, j * H:(j + 1) * H], ident[:, :])
                ins.then_inc(s_tr, 1)
            turn(0, True)
            turn_back(0)
            for c in range(PAIR_CHUNKS):
                layer0(0, c, True)
            pe.wait_ge(s_tr_hi, GROUPS)
            pe.wait_ge(s_tr_lo, CHUNKS)
            step(0, first=True)
            with pe.Fori(1, NBLOCKS - 1) as i:
                step(i)
            step(NBLOCKS - 1, last=True)
            for at in left(LAG_G2):
                form_g2(*at)
            pe.wait_ge(s_dense, 16)
            for t in range(BTILES):
                ins = nc.tensor.transpose(side[0:D, t * P:(t + 1) * P], dense_raw[:, t, :], ident[:, :])
            ins.then_inc(s_dense_t, 1)
            pe.wait_ge(s_g2e, NBLOCKS * TILES)
            pe.wait_ge(s_mul, NBLOCKS * TILES * MUL_TILE)
            pe.wait_ge(s_stt, NBLOCKS * TILES * STT_TILE)
            for j in range(F):
                ins = nc.tensor.matmul(v[:, 0, :], w2_t[:, j * H:(j + 1) * H], g2[:, j, :], start=(j == 0),
                                       stop=(j == F - 1))
            ins.then_inc(s_z3, 1)
            pe.wait_ge(s_top, 48)
            pe.wait_ge(s_z1, NBLOCKS)
            pe.wait_ge(s_dense_t, 2)
            for c in range(4):
                cols = slice(c * P, (c + 1) * P)
                if c >= 2:
                    pe.wait_ge(s_m1e, c - 1)
                out = v[:, 3 + c % 2, :]
                nc.tensor.matmul(out, wt1_dense[:, cols], dense_t[:, :], start=True, stop=False)
                nc.tensor.matmul(out, wt1[:, 0, cols], z1[:, :], start=False, stop=False)
                nc.tensor.matmul(out, wt1[:, 1, cols], g2[:, F, :], start=False, stop=False)
                if c == 0:
                    pe.wait_ge(s_z3e, 1)
                nc.tensor.matmul(out, wt1[:, 2, cols], z3[:, :], start=False, stop=True).then_inc(s_m1, 1)
            for c in range(2):
                for k in range(4):
                    if c == 0:
                        pe.wait_ge(s_m1e, k + 1)
                    ins = nc.tensor.matmul(v[:, 1 + c, :], wt2[:, k, c * P:(c + 1) * P], h1[:, k, :], start=(k == 0),
                                           stop=(k == 3))
                ins.then_inc(s_m2, 1)
            for k in range(2):
                pe.wait_ge(s_m2e, k + 1)
                ins = nc.tensor.matmul(x1_ps[0:1, :], wt3[:, k:k + 1], h2[:, k, :], start=(k == 0), stop=(k == 1))
            ins.then_inc(s_y, 1)


def constants():
    ident = np.eye(P, dtype=np.float32)
    mask = np.zeros((P, TILE_B), np.float32)
    for p in range(P):
        mask[p, p // D] = 1.0
    return ident, mask


def kernel(**inputs):
    import concourse.bacc as bacc
    from concourse.bass_utils import run_bass_kernel_spmd as run

    nc = bacc.Bacc("TRN2", target_bir_lowering=False, num_devices=1)
    arrays = {}

    def given(name, a):
        a = np.ascontiguousarray(a)
        arrays[f"in_{name}_dram"] = a
        return nc.dram_tensor(f"in_{name}_dram", a.shape, mybir.dt.from_np(a.dtype), kind="ExternalInput").ap()

    ids = given("ids", inputs["ids"])
    tables = [given(f"tbl_{j}", inputs[f"tbl_{j}"]) for j in range(F)]
    rest = [given(k, inputs[k]) for k in ("dense_ctx", "W_top1", "b_top1", "W_top2", "b_top2", "W_top3",
                                          "L0_rec_W0", "L0_rec_b0", "L0_rec_W1", "L0_rec_b1",
                                          "L0_rec_W2", "L0_rec_b2")]
    fixed = [given(k, a) for k, a in zip(("ident", "mask"), constants())]
    y = nc.dram_tensor("out_y_dram", (B, 1), F32, kind="ExternalOutput").ap()
    bass_dlrm(nc, ids, tables, *rest, *fixed, y)
    r = run(nc, [arrays], core_ids=[0])
    return r.results[0]["out_y_dram"]
```

```python
from contextlib import ExitStack

import numpy as np
import concourse.bass as bass
from concourse import mybir

ALU = mybir.AluOpType
ACT = mybir.ActivationFunctionType
AX_X = mybir.AxisListType.X
F32 = mybir.dt.float32
F32R = mybir.dt.float32r
I32 = mybir.dt.int32

P = 128
B, F, D = 512, 39, 16
H = 128
NDELTA = (F + 1) // 2
PER_CHUNK = 3
PAIR_CHUNKS = -(-NDELTA // PER_CHUNK)
PAIRS = PER_CHUNK * F
SPLIT = [1, 4]
WHOLE = [c for c in range(PAIR_CHUNKS) if c not in SPLIT]
XROWS = 2 * F
BLOCK_B = 32
NBLOCKS = B // BLOCK_B
COLS = BLOCK_B * D
TILE_B = P // D
TILES = COLS // P
BTILES = B // P
FE = F + 1
JC = 4
CHUNKS = -(-F // JC)
SLOTS = TILES * CHUNKS
VBANKS = 5
SHORT = 8
STARTS = [c * JC - (CHUNKS * JC - F) * (c > SHORT) for c in range(CHUNKS)] + [F]
FIELDS = [list(range(STARTS[c], STARTS[c + 1])) for c in range(CHUNKS)]

ACT_CHUNKS = [1, 3, 5, 7, 9]
DVE_CHUNKS = [c for c in range(CHUNKS) if c not in ACT_CHUNKS]
STT_TILE = sum(len(FIELDS[c]) for c in DVE_CHUNKS) + 1
MUL_TILE = sum(len(FIELDS[c]) for c in ACT_CHUNKS)
NPROD = len(ACT_CHUNKS)
SUMS = NPROD - 2
POOL_TILE = 1 + SUMS + 1
POOL_BLOCK = TILES * POOL_TILE
X2_TILE = 2
SIDE = 2

S_TURN, S_TURNED, S_BACK, S_BACKED = 1, 2, 4, 5
QUAD_AT = [9, 12, 15, 18, 21, 24, 27]
HI_AT, LO_AT = [13, 22], [14, 24]
L0_AT = [13, 17, 19, 22, 27, 29, 32]
S_X1 = 32
FOLD = 6
LAG_X2, LAG_G2, LAG_G2E = 6, 9, 10
X1_PARTS = [(0, COLS - P), (COLS - P, COLS)]

PLAIN = JC
HI_RING = 4
W2_AHEAD = 4
LO_POOL = JC - 1
NBIAS = 11
GATHERED_EARLY = F + 3
FIRST_POOL = 4
GATHERED_FIRST = F + 15


def bass_dlrm(nc, ids, tables, dense, w_top1, b_top1, w_top2, b_top2, w_top3,
              w0, b0, w1, b1, w2, b2, ident_c, mask_c, y):
    ctx = ExitStack()
    with ctx:
        def sb(name, shape, dt=F32, stack=ctx):
            return stack.enter_context(nc.sbuf_tensor(name, shape, dt))

        def sem(name):
            return ctx.enter_context(nc.semaphore(name))

        early = ExitStack()
        w0_raw = sb("w0_raw", [P, F * F], F32, early)
        w0_sym = sb("w0_sym", [P, NDELTA, F], F32, early)
        w1_raw = sb("w1_raw", [P, F * H], F32, early)
        w2_raw = sb("w2_raw", [P, F * H], F32, early)
        early.close()
        whole = ExitStack()
        g2 = sb("g2", [P, FE, B], F32, whole)
        whole.close()
        g2_lo = sb("g2_lo", [P, FE, B], F32R)

        middle = ExitStack()
        w1_hi = sb("w1_hi", [P, F * H], F32R, middle)
        w1_lo = sb("w1_lo", [P, F * H], F32R, middle)
        middle.close()
        late_use = ExitStack()
        w2_hi = sb("w2_hi", [P, F * H], F32R, late_use)
        g2_hi = sb("g2_hi", [P, HI_RING, B], F32R, late_use)
        h1 = sb("h1", [P, 4, B], F32, late_use)
        z3 = sb("z3", [P, B], F32, late_use)
        late_use.close()
        sb("w1_place", [P, 2 * F * H])

        ids_sb = sb("ids_sb", [P, BTILES, F], I32)
        emb = sb("emb", [P, BTILES, F * D])
        emb_block = sb("emb_block", [P, 2, F * D])
        ident = sb("ident", [P, P])
        mask = sb("mask", [P, TILE_B])
        w0_t = sb("w0_t", [PAIRS, len(WHOLE), H])
        w0_hi = sb("w0_hi", [PAIRS, len(SPLIT), H], F32R)
        w0_lo = sb("w0_lo", [PAIRS, len(SPLIT), H], F32R)
        whole = ExitStack()
        w2_t = sb("w2_t", [P, F * H], F32, whole)
        whole.close()
        w2_lo = sb("w2_lo", [P, F * H], F32R)
        x0_use = ExitStack()
        x0 = sb("x0", [XROWS, COLS], F32, x0_use)
        x0_use.close()
        y_row = sb("y_row", [1, B])
        x0_rep = sb("x0_rep", [PAIRS, COLS])
        pairs_use = ExitStack()
        quad = sb("quad", [PAIRS, PAIR_CHUNKS, COLS], F32, pairs_use)
        pairs_use.close()
        in_place = ExitStack()
        quad_lo = sb("quad_lo", [PAIRS, PAIR_CHUNKS, COLS], F32R, in_place)
        in_place.close()
        top_use = ExitStack()
        wt1 = sb("wt1", [P, 3, 512], F32, top_use)
        wt1_dense = sb("wt1_dense", [D, 512], F32, top_use)
        wt2 = sb("wt2", [P, 4, 256], F32, top_use)
        dense_t = sb("dense_t", [D, B], F32, top_use)
        top_use.close()
        sb("quad_place", [P, PAIR_CHUNKS * COLS])
        quad_hi = sb("quad_hi", [PAIRS, COLS], F32R)
        dense_raw = sb("dense_raw", [P, BTILES, D])
        x0_t_next = sb("x0_t_next", [P, TILES, F])
        x0_t = sb("x0_t", [P, TILES, FE])
        x1 = sb("x1", [P, COLS])
        parts_use = ExitStack()
        x1_hi = sb("x1_hi", [P, COLS], F32R, parts_use)
        x1_lo = sb("x1_lo", [P, COLS], F32R, parts_use)
        parts_use.close()
        h2 = sb("h2", [P, 2, B])
        acc = sb("acc", [P, 2, 2, H])
        prod = sb("prod", [P, NPROD, JC * H])
        partial = sb("partial", [P, JC * H])
        x2_t = sb("x2_t", [P, 2, H])
        spread = sb("spread", [P, 2, TILE_B * FE])
        b0_sb = sb("b0_sb", [P, 1])
        b1_row = sb("b1_row", [P, H])
        b2_sb = sb("b2_sb", [P, 1])
        b2_x16 = sb("b2_x16", [P, 1])
        bt1_sb = sb("bt1_sb", [P, 4])
        bt2_sb = sb("bt2_sb", [P, 2])
        wt3 = sb("wt3", [P, 2])
        z1 = sb("z1", [P, B])

        v = ctx.enter_context(nc.psum_tensor("v", [P, VBANKS, 512], F32))
        side = ctx.enter_context(nc.psum_tensor("side", [P, 512], F32))
        x1_ps = ctx.enter_context(nc.psum_tensor("x1_ps", [P, COLS], F32))
        g2_ps = ctx.enter_context(nc.psum_tensor("g2_ps", [P, 512], F32))

        top_ps = [v[:, 0, :], g2_ps]

        def pairs(c):
            return min(PER_CHUNK, NDELTA - PER_CHUNK * c) * F

        s_ids, s_w0, s_w1, s_w2 = sem("s_ids"), sem("s_w0"), sem("s_w1"), sem("s_w2")
        s_const, s_bias, s_dense = sem("s_const"), sem("s_bias"), sem("s_dense")
        s_gathered = sem("s_gathered")
        s_block = sem("s_block")
        s_top = sem("s_top")
        s_out = sem("s_out")
        s_zeroed = sem("s_zeroed")
        s_sym = sem("s_sym")
        s_tr = sem("s_tr")
        s_tr_hi = sem("s_tr_hi")
        s_tr_lo = sem("s_tr_lo")
        s_scaled = sem("s_scaled")
        s_side = sem("s_side")
        s_x0 = sem("s_x0")
        s_rep = sem("s_rep")
        s_pair = [sem(f"s_pair{c}") for c in range(PAIR_CHUNKS)]
        s_pair_first = [sem(f"s_pair_first{c}") for c in range(FIRST_POOL, PAIR_CHUNKS)]
        s_x0t = sem("s_x0t")
        s_quad = sem("s_quad")
        s_qhi = sem("s_qhi")
        s_qlo = sem("s_qlo")
        s_l0 = sem("s_l0")
        s_x1 = sem("s_x1")
        s_x1h = sem("s_x1h")
        s_x1l = sem("s_x1l")
        s_z1 = sem("s_z1")
        s_cur = sem("s_cur")
        s_v = sem("s_v")
        s_stt = sem("s_stt")
        s_mul = sem("s_mul")
        s_pool = sem("s_pool")
        s_fold = sem("s_fold")
        s_x2 = sem("s_x2")
        s_dense_t = sem("s_dense_t")
        s_g2 = sem("s_g2")
        s_g2e = sem("s_g2e")
        s_w2hi, s_w2lo = sem("s_w2hi"), sem("s_w2lo")
        s_ghi = sem("s_ghi")
        s_glo = sem("s_glo")
        s_glo_pool = sem("s_glo_pool")
        s_z3 = sem("s_z3")
        s_z3e = sem("s_z3e")
        s_m1, s_m1e = sem("s_m1"), sem("s_m1e")
        s_m2, s_m2e = sem("s_m2"), sem("s_m2e")
        s_y, s_ye = sem("s_y"), sem("s_ye")

        SPLIT_FIELDS = range(PLAIN, F)
        W1_GROUP0 = 3
        W2_GROUP0 = W1_GROUP0 + CHUNKS
        GROUPS = W2_GROUP0 + CHUNKS
        W0_GROUPS = [WHOLE[:4], WHOLE[4:], SPLIT]
        LO_GROUPS = 1 + CHUNKS

        def stt_done(g):
            t, c = divmod(g, CHUNKS)
            return STT_TILE * t + sum(len(FIELDS[x]) for x in DVE_CHUNKS if x <= c)

        def mul_done(g):
            t, c = divmod(g, CHUNKS)
            return MUL_TILE * t + sum(len(FIELDS[x]) for x in ACT_CHUNKS if x <= c)

        def late(n, g, lag, first):
            t, off = divmod(g - lag, CHUNKS)
            if off or (first and t < 1):
                return []
            return [(n, t - 1)] if t >= 1 else [(n - 1, t - 1 + TILES)]

        def left(lag):
            return [(NBLOCKS - 1, t) for t in range(TILES) if CHUNKS * (t + 1) + lag >= SLOTS]

        def pool_done(t, step):
            return POOL_TILE * t + 1 + step

        def copy_rep(engine):
            for r in range(PER_CHUNK):
                engine.dma_start(x0_rep[r * F:(r + 1) * F, :], x0[0:F, :]).then_inc(s_rep, 16)

        def copy_pairs(engine, chunks, arrived):
            for c, s_arrived in zip(chunks, arrived):
                for r in range(pairs(c) // F):
                    delta = PER_CHUNK * c + r
                    engine.dma_start(quad[r * F:(r + 1) * F, c, :], x0[delta:delta + F, :]).then_inc(s_arrived, 16)

        block = ctx.enter_context(nc.Block())

        @block.sync
        def _(sp):
            sp.dma_start(ids_sb[:, :, :], ids.rearrange("(t p) f -> p t f", p=P)).then_inc(s_ids, 16)
            sp.dma_start(w0_raw[:, :], w0).then_inc(s_w0, 16)
            sp.dma_start(ident[:, :], ident_c).then_inc(s_const, 16)
            sp.dma_start(mask[:, :], mask_c).then_inc(s_const, 16)
            sp.dma_start(w1_raw[:, :], w1).then_inc(s_w1, 16)
            sp.dma_start(b0_sb[:, :], b0.rearrange("(h o) -> h o", o=1)).then_inc(s_bias, 16)
            sp.dma_start(b2_sb[:, :], b2.rearrange("(h o) -> h o", o=1)).then_inc(s_bias, 16)
            sp.dma_start(b1_row[:, :], b1.rearrange("(o h) -> o h", o=1).broadcast_to([P, H])).then_inc(s_bias, 16)
            for c in range(4):
                sp.dma_start(bt1_sb[:, c:c + 1], b_top1[c * P:(c + 1) * P].rearrange("(h o) -> h o", o=1)).then_inc(s_bias, 16)
            for c in range(2):
                sp.dma_start(bt2_sb[:, c:c + 1], b_top2[c * P:(c + 1) * P].rearrange("(h o) -> h o", o=1)).then_inc(s_bias, 16)
                sp.dma_start(wt3[:, c:c + 1], w_top3[c * P:(c + 1) * P, :]).then_inc(s_bias, 16)
            sp.dma_start(w2_raw[:, :], w2).then_inc(s_w2, 16)

            def stage(t, q):
                if q == 0:
                    sp.wait_ge(s_gathered, t * (16 * F) + 16 * F)
                for half in range(2):
                    sp.dma_start(emb_block[0:BLOCK_B, half, :],
                                 emb[q * BLOCK_B:(q + 1) * BLOCK_B, t, :]).then_inc(s_block, 16)
                sp.wait_ge(s_x0, t * (P // BLOCK_B) + q + 1)
                copy_rep(sp)
                copy_pairs(sp, range(PAIR_CHUNKS), s_pair)

            sp.wait_ge(s_zeroed, 1)
            sp.wait_ge(s_x0, 1)
            copy_rep(sp)
            copy_pairs(sp, range(FIRST_POOL), s_pair)
            for q in range(1, P // BLOCK_B):
                stage(0, q)
            with sp.Fori(1, BTILES) as t:
                for q in range(P // BLOCK_B):
                    stage(t, q)
            sp.dma_start(dense_raw[:, :, :], dense.rearrange("(t p) f -> p t f", p=P)).then_inc(s_dense, 16)
            sp.wait_ge(s_l0, PAIR_CHUNKS * NBLOCKS)
            sp.dma_start(wt1[:, :, :], w_top1[0:3 * P, :].rearrange("(c p) m -> p c m", p=P)).then_inc(s_top, 16)
            sp.dma_start(wt1_dense[:, :], w_top1[3 * P:3 * P + D, :]).then_inc(s_top, 16)
            sp.dma_start(wt2[:, :, :], w_top2.rearrange("(c p) m -> p c m", p=P)).then_inc(s_top, 16)
            sp.wait_ge(s_ye, 1)
            sp.dma_start(y.rearrange("b o -> o b"), y_row[:, :]).then_inc(s_out, 16)
            sp.wait_ge(s_out, 16)

        @block.gpsimd
        def _(pool):
            order = [(t, j) for t in range(BTILES) for j in range(F)]

            def gather(n):
                for t, j in order[:n]:
                    if j == 0 and t > 0:
                        pool.wait_ge(s_gathered, 16 * F * t)
                    nc.gpsimd.indirect_dma_start(
                        emb[:, t, j * D:(j + 1) * D], None, tables[j],
                        bass.IndirectOffsetOnAxis(ids_sb[:, t, j:j + 1], 0)).then_inc(s_gathered, 16)
                del order[:n]

            def x1_split_lo(m, part):
                a, b = X1_PARTS[part]
                pool.wait_ge(s_x1h, 2 * m + part + 1)
                nc.gpsimd.tensor_tensor(x1_lo[:, a:b], x1[:, a:b], x1_hi[:, a:b].bitcast(F32),
                                        ALU.subtract).then_inc(s_x1l, 1)

            def spread_x0(n, t, first):
                if t == 0:
                    pool.wait_ge(s_cur, n + 1)
                if not (first and t < 2):
                    pool.wait_ge(s_g2, n * TILES + t - 1)
                nc.gpsimd.tensor_tensor(
                    spread[:, t % 2, :].rearrange("p (b j) -> p b j", b=TILE_B),
                    mask[:, :].unsqueeze(2).broadcast_to([P, TILE_B, FE]),
                    x0_t[:, t, :].unsqueeze(1).broadcast_to([P, TILE_B, FE]), ALU.mult).then_inc(s_pool, 1)

            def sum_tile(n, t):
                base, muls = n * POOL_BLOCK, n * (TILES * MUL_TILE)
                for k in range(1, SUMS + 1):
                    w = len(FIELDS[ACT_CHUNKS[k + 1]]) * H
                    pool.wait_ge(s_pool, base + pool_done(t, k - 1))
                    if k == 1:
                        if not (isinstance(n, int) and n == 0 and t == 0):
                            pool.wait_ge(s_x2, (n * TILES + t) * X2_TILE)
                        pool.wait_ge(s_fold, n * TILES + t + 1)
                    pool.wait_ge(s_mul, muls + mul_done(t * CHUNKS + ACT_CHUNKS[k + 1]))
                    nc.gpsimd.tensor_tensor(partial[:, 0:w], prod[:, 0, :] if k == 1 else partial[:, 0:w],
                                            prod[:, k + 1, 0:w], ALU.add).then_inc(s_pool, 1)
                pool.wait_ge(s_pool, base + pool_done(t, SUMS))
                nc.gpsimd.tensor_tensor(partial[:, 0:2 * H], partial[:, 0:2 * H], partial[:, 2 * H:4 * H],
                                        ALU.add).then_inc(s_pool, 1)

            pool.wait_ge(s_ids, 16)
            gather(GATHERED_EARLY)
            pool.wait_ge(s_x0, 1)
            copy_pairs(pool, range(FIRST_POOL, PAIR_CHUNKS), s_pair_first)
            gather(GATHERED_FIRST - GATHERED_EARLY)
            pool.wait_ge(s_const, 32)

            def step(n, first=False, last=False, gathers=0):
                for t in range(TILES):
                    spread_x0(n, t, first)
                    if t == 1 and not first:
                        x1_split_lo(n, 1)
                    sum_tile(n, t)
                    if t == TILES - 2 and not last:
                        x1_split_lo(n + 1, 0)
                    gather(gathers + t % 2 if gathers else 0)

            n = 0
            while order:
                step(n, first=(n == 0), gathers=2)
                n += 1
            with pool.Fori(n, NBLOCKS - 1) as i:
                step(i)
            step(NBLOCKS - 1, last=True)
            for j in SPLIT_FIELDS:
                if j % JC == LO_POOL:
                    pool.wait_ge(s_ghi, j - PLAIN + 1)
                    nc.gpsimd.tensor_tensor(g2_lo[:, j, :], g2[:, j, :], g2_hi[:, j % HI_RING, :].bitcast(F32),
                                            ALU.subtract).then_inc(s_glo_pool, 1)

        @block.scalar
        def _(act):
            def copy_x0(m, first):
                act.wait_ge(s_side, m * SIDE + 1)
                if not first:
                    act.wait_ge(s_l0, m * PAIR_CHUNKS)
                nc.scalar.activation(x0[:, :].rearrange("p (b d) -> p d b", d=D),
                                     side[0:XROWS, :].rearrange("p (d b) -> p d b", d=D),
                                     ACT.Copy).then_inc(s_x0, 1)

            def copy_x0_t(m, first):
                act.wait_ge(s_side, m * SIDE + 2)
                if not first:
                    act.wait_ge(s_cur, m)
                nc.scalar.activation(x0_t_next[:, :, :],
                                     side[:, 0:TILES * XROWS].rearrange("p (t j) -> p t j", j=XROWS)[:, :, 0:F],
                                     ACT.Copy).then_inc(s_x0t, 1)

            def move_x0_t(n, first):
                act.wait_ge(s_x0t, n + 1)
                if first:
                    act.wait_ge(s_zeroed, 2)
                else:
                    act.wait_ge(s_mul, n * (TILES * MUL_TILE))
                    act.wait_ge(s_stt, n * (TILES * STT_TILE))
                    act.wait_ge(s_pool, n * POOL_BLOCK + pool_done(TILES - 1, 0) - POOL_BLOCK)
                nc.scalar.activation(x0_t[:, :, 0:F], x0_t_next[:, :, :], ACT.Copy).then_inc(s_cur, 1)

            def split_hi(m, c):
                i, w = SPLIT.index(c), pairs(c)
                act.wait_ge(s_quad, PAIR_CHUNKS * m + c + 1)
                if i > 0:
                    act.wait_ge(s_l0, PAIR_CHUNKS * m + SPLIT[i - 1] + 1)
                nc.scalar.activation(quad_hi[0:w, :], quad[0:w, c, :], ACT.Copy).then_inc(s_qhi, 1)

            def copy_x1(m, first):
                act.wait_ge(s_l0, PAIR_CHUNKS * (m + 1))
                if not first:
                    act.wait_ge(s_x1l, 2 * m)
                    act.wait_ge(s_z1, m)
                nc.scalar.activation(x1[:, :], x1_ps[:, :], ACT.Identity, bias=b0_sb[:, 0:1]).then_inc(s_x1, 1)

            def x1_split_hi(m, part, first):
                a, b = X1_PARTS[part]
                act.wait_ge(s_x1, m + 1)
                if not first:
                    act.wait_ge(s_v, SLOTS * m - SLOTS + CHUNKS * (b // P))
                nc.scalar.activation(x1_hi[:, a:b], x1[:, a:b], ACT.Copy).then_inc(s_x1h, 1)

            def products(n, g, first):
                t, c = divmod(g, CHUNKS)
                k = ACT_CHUNKS.index(c)
                if g == ACT_CHUNKS[0]:
                    act.wait_ge(s_cur, n + 1)
                if not (first and t == 0):
                    if k == 1:
                        act.wait_ge(s_fold, n * TILES + t)
                    else:
                        act.wait_ge(s_pool, n * POOL_BLOCK + pool_done(t - 1, max(k - 1, 1)))
                act.wait_ge(s_v, n * SLOTS + g + 1)
                for x, j in enumerate(FIELDS[c]):
                    nc.scalar.activation(prod[:, k, x * H:(x + 1) * H], v[:, g % VBANKS, x * H:(x + 1) * H],
                                         ACT.Copy, scale=x0_t[:, t, j:j + 1]).then_inc(s_mul, 1)

            def copy_g2(n, t):
                b_at = n * BLOCK_B + t * TILE_B
                act.wait_ge(s_g2, n * TILES + t + 1)
                act.wait_ge(s_tr_hi, GROUPS)
                nc.scalar.activation(g2[:, :, bass.ds(b_at, TILE_B)],
                                     g2_ps[:, 0:TILE_B * FE].rearrange("p (b j) -> p j b", b=TILE_B),
                                     ACT.Copy).then_inc(s_g2e, 1)

            def step(n, first=False, last=False):
                for g in range(SLOTS):
                    if g == 0:
                        move_x0_t(n, first)
                        if not first:
                            x1_split_hi(n, 1, False)
                    if not last:
                        m = n + 1
                        if g == S_BACKED:
                            copy_x0_t(m, False)
                        if g == S_TURNED:
                            copy_x0(m, False)
                        if g in HI_AT:
                            split_hi(m, SPLIT[HI_AT.index(g)])
                        if g == S_X1:
                            copy_x1(m, False)
                            x1_split_hi(m, 0, False)
                    for at in late(n, g, LAG_G2E, first):
                        copy_g2(*at)
                    if g % CHUNKS in ACT_CHUNKS:
                        products(n, g, first)

            for s in range(GROUPS):
                act.wait_ge(s_tr, s + 1)
                bank = v[:, s % VBANKS, :]
                if s < 3:
                    rows, w = pairs(W0_GROUPS[s][0]), len(W0_GROUPS[s]) * H
                    dst = [w0_t[0:rows, 0:4, :], w0_t[0:rows, 4:, :], w0_hi[0:rows, :, :]][s]
                    nc.scalar.activation(dst.rearrange("p c h -> p (c h)"), bank[0:rows, 0:w],
                                         ACT.Copy).then_inc(s_tr_hi, 1)
                else:
                    dst, c = (w1_hi, s - W1_GROUP0) if s < W2_GROUP0 else (w2_t, s - W2_GROUP0)
                    w = len(FIELDS[c]) * H
                    nc.scalar.activation(dst[:, STARTS[c] * H:STARTS[c] * H + w], bank[:, 0:w], ACT.Copy).then_inc(s_tr_hi, 1)
            act.wait_ge(s_bias, 16 * NBIAS)
            nc.scalar.mul(b2_x16[:, :], b2_sb[:, :], float(D)).then_inc(s_scaled, 1)
            act.wait_ge(s_gathered, 16 * F)
            act.wait_ge(s_zeroed, 1)
            nc.scalar.activation(emb_block[0:BLOCK_B, 1, :], emb[0:BLOCK_B, 0, :], ACT.Copy).then_inc(s_block, 16)
            copy_x0(0, True)
            copy_x0_t(0, True)
            for c in SPLIT:
                split_hi(0, c)
            copy_x1(0, True)
            for part in range(2):
                x1_split_hi(0, part, True)
            step(0, first=True)
            with act.Fori(1, NBLOCKS - 1) as i:
                step(i)
            step(NBLOCKS - 1, last=True)
            act.wait_ge(s_dense_t, 1)
            nc.scalar.activation(dense_t[:, :], side[0:D, :], ACT.Copy).then_inc(s_dense_t, 1)
            act.wait_ge(s_v, SLOTS * NBLOCKS)

            def w2_part(c):
                a, w = c * JC * H, min(JC, F - c * JC) * H
                nc.scalar.activation(w2_hi[:, a:a + w], w2_t[:, a:a + w], ACT.Copy).then_inc(s_w2hi, 1)

            for c in range(1, W2_AHEAD):
                w2_part(c)
            for at in left(LAG_G2E):
                copy_g2(*at)
            act.wait_ge(s_g2e, NBLOCKS * TILES)
            for j in SPLIT_FIELDS:
                if j % JC == 0 and j // JC >= W2_AHEAD:
                    w2_part(j // JC)
                if j - HI_RING >= PLAIN:
                    act.wait_ge(s_z3, j - HI_RING + 1)
                nc.scalar.activation(g2_hi[:, j % HI_RING, :], g2[:, j, :], ACT.Copy).then_inc(s_ghi, 1)
            act.wait_ge(s_scaled, 1)
            act.wait_ge(s_z3, F)
            nc.scalar.activation(z3[:, :], x1_ps[:, :], ACT.Identity, bias=b2_x16[:, 0:1]).then_inc(s_z3e, 1)
            for c in range(4):
                act.wait_ge(s_m1, c + 1)
                nc.scalar.activation(h1[:, c, :], v[:, 1 + c, :], ACT.Relu, bias=bt1_sb[:, c:c + 1]).then_inc(s_m1e, 1)
            for c in range(2):
                act.wait_ge(s_m2, c + 1)
                nc.scalar.activation(h2[:, c, :], top_ps[c][:, :], ACT.Relu, bias=bt2_sb[:, c:c + 1]).then_inc(s_m2e, 1)
            act.wait_ge(s_y, 1)
            nc.scalar.activation(y_row[:, :], side[0:1, :], ACT.Copy).then_inc(s_ye, 1)

        @block.vector
        def _(dve):
            def pair_products(m, c, first=False):
                w = pairs(c)
                each = 16 * w // F
                if c == 0:
                    dve.wait_ge(s_rep, m * (16 * PER_CHUNK) + 16 * PER_CHUNK)
                if c < FIRST_POOL:
                    dve.wait_ge(s_pair[c], m * each + each)
                elif first:
                    dve.wait_ge(s_pair_first[c - FIRST_POOL], each)
                else:
                    dve.wait_ge(s_pair[c], m * each)
                nc.vector.tensor_tensor(quad[0:w, c, :], quad[0:w, c, :], x0_rep[0:w, :], ALU.mult).then_inc(s_quad, 1)

            def split_lo(m, c):
                w = pairs(c)
                dve.wait_ge(s_qhi, len(SPLIT) * m + SPLIT.index(c) + 1)
                nc.vector.tensor_tensor(quad_lo[0:w, c, :], quad[0:w, c, :], quad_hi[0:w, :].bitcast(F32),
                                        ALU.subtract).then_inc(s_qlo, 1)

            def sum_x1(m):
                dve.wait_ge(s_x1, m + 1)
                nc.vector.tensor_reduce(z1[:, bass.ds(m * BLOCK_B, BLOCK_B)],
                                        x1[:, :].rearrange("p (b d) -> p b d", d=D), AX_X,
                                        ALU.add).then_inc(s_z1, 1)

            def sums(n, g, first):
                t, c = divmod(g, CHUNKS)
                base = n * (TILES * STT_TILE) + t * STT_TILE
                k = sum(len(FIELDS[x]) for x in DVE_CHUNKS if x < c)
                if g == 0:
                    dve.wait_ge(s_cur, n + 1)
                if k == 0 and not (first and t < 2):
                    dve.wait_ge(s_x2, (n * TILES + t - 1) * X2_TILE)
                dve.wait_ge(s_v, n * SLOTS + g + 1)
                for x, j in enumerate(FIELDS[c]):
                    into, term, weight = acc[:, t % 2, k % 2, :], v[:, g % VBANKS, x * H:(x + 1) * H], x0_t[:, t, j:j + 1]
                    if k >= 2:
                        dve.wait_ge(s_stt, base + k - 1)
                    if k == 1:
                        nc.vector.tensor_scalar(into, term, weight, None, ALU.mult).then_inc(s_stt, 1)
                    else:
                        nc.vector.scalar_tensor_tensor(out=into, in0=term, scalar=weight,
                                                       in1=b1_row[:, :] if k == 0 else into,
                                                       op0=ALU.mult, op1=ALU.add).then_inc(s_stt, 1)
                    k += 1
                if c == DVE_CHUNKS[-1]:
                    dve.wait_ge(s_stt, base + k)
                    nc.vector.tensor_tensor(acc[:, t % 2, 0, :], acc[:, t % 2, 0, :], acc[:, t % 2, 1, :],
                                            ALU.add).then_inc(s_stt, 1)

            def fold(n, t):
                dve.wait_ge(s_mul, n * (TILES * MUL_TILE) + mul_done(t * CHUNKS + ACT_CHUNKS[1]))
                nc.vector.tensor_tensor(prod[:, 0, :], prod[:, 0, :], prod[:, 1, :], ALU.add).then_inc(s_fold, 1)

            def finish_x2(n, t):
                slot = t % 2
                dve.wait_ge(s_stt, (n * TILES + t + 1) * STT_TILE)
                dve.wait_ge(s_pool, n * POOL_BLOCK + pool_done(t, SUMS + 1))
                nc.vector.tensor_tensor(acc[:, slot, 0, :], acc[:, slot, 0, :], partial[:, 0:H],
                                        ALU.add).then_inc(s_x2, 1)
                dve.wait_ge(s_x2, (n * TILES + t) * X2_TILE + 1)
                if not (isinstance(n, int) and n == 0 and t < 2):
                    dve.wait_ge(s_g2, n * TILES + t - 1)
                nc.vector.tensor_tensor(x2_t[:, slot, :], acc[:, slot, 0, :], partial[:, H:2 * H],
                                        ALU.add).then_inc(s_x2, 1)

            def step(n, first=False, last=False):
                for g in range(SLOTS):
                    if not last:
                        m = n + 1
                        if g in QUAD_AT:
                            pair_products(m, QUAD_AT.index(g))
                        if g in LO_AT:
                            split_lo(m, SPLIT[LO_AT.index(g)])
                        if g == S_X1 + 1:
                            sum_x1(m)
                    if g % CHUNKS == FOLD:
                        fold(n, g // CHUNKS)
                    for at in late(n, g, LAG_X2, first):
                        finish_x2(*at)
                    if g % CHUNKS in DVE_CHUNKS:
                        sums(n, g, first)

            nc.vector.memset(emb_block[:, :, :], 0.0).then_inc(s_zeroed, 1)
            nc.vector.memset(x0_t[:, :, F:FE], 1.0).then_inc(s_zeroed, 1)
            dve.wait_ge(s_w0, 16)
            nc.vector.tensor_copy(w0_sym[:, 0, :], w0_raw[:, 0:F * F:F + 1])
            for delta in range(1, NDELTA):
                for j0, j1, wrap in ((0, F - delta, 0), (F - delta, F, F)):
                    a = j0 * (F + 1) + delta - wrap
                    b = j0 * (F + 1) + F * delta - F * wrap
                    last_row = (j1 - j0 - 1) * (F + 1) + 1
                    ins = nc.vector.tensor_tensor(w0_sym[:, delta, j0:j1], w0_raw[:, a:a + last_row:F + 1],
                                                  w0_raw[:, b:b + last_row:F + 1], ALU.add)
            ins.then_inc(s_sym, 1)
            dve.wait_ge(s_tr_hi, 3)
            nc.vector.tensor_tensor(w0_lo[:, :, :].rearrange("p c h -> p (c h)"), v[0:PAIRS, 2, 0:len(SPLIT) * H],
                                    w0_hi[:, :, :].rearrange("p c h -> p (c h)").bitcast(F32),
                                    ALU.subtract).then_inc(s_tr_lo, 1)
            for c in range(CHUNKS):
                a, w = STARTS[c] * H, len(FIELDS[c]) * H
                dve.wait_ge(s_tr_hi, W1_GROUP0 + c + 1)
                nc.vector.tensor_tensor(w1_lo[:, a:a + w], v[:, (W1_GROUP0 + c) % VBANKS, 0:w],
                                        w1_hi[:, a:a + w].bitcast(F32), ALU.subtract).then_inc(s_tr_lo, 1)
            dve.wait_ge(s_bias, 16 * NBIAS)
            dve.wait_ge(s_gathered, 16 * F)
            dve.wait_ge(s_zeroed, 1)
            nc.vector.tensor_copy(emb_block[0:BLOCK_B, 0, :], emb[0:BLOCK_B, 0, :]).then_inc(s_block, 16)
            for c in range(PAIR_CHUNKS):
                pair_products(0, c, first=True)
                if c in SPLIT:
                    split_lo(0, c)
            for part, (a, b) in enumerate(X1_PARTS):
                dve.wait_ge(s_x1h, part + 1)
                nc.vector.tensor_tensor(x1_lo[:, a:b], x1[:, a:b], x1_hi[:, a:b].bitcast(F32),
                                        ALU.subtract).then_inc(s_x1l, 1)
            sum_x1(0)
            step(0, first=True)
            with dve.Fori(1, NBLOCKS - 1) as i:
                step(i)
            step(NBLOCKS - 1, last=True)
            for at in left(LAG_X2):
                finish_x2(*at)
            for j in SPLIT_FIELDS:
                c = j // JC
                if j % JC == 0:
                    a, w = c * JC * H, min(JC, F - c * JC) * H
                    dve.wait_ge(s_w2hi, c)
                    nc.vector.tensor_tensor(w2_lo[:, a:a + w], w2_t[:, a:a + w], w2_hi[:, a:a + w].bitcast(F32),
                                            ALU.subtract).then_inc(s_w2lo, 1)
                if j % JC != LO_POOL:
                    dve.wait_ge(s_ghi, j - PLAIN + 1)
                    nc.vector.tensor_tensor(g2_lo[:, j, :], g2[:, j, :], g2_hi[:, j % HI_RING, :].bitcast(F32),
                                            ALU.subtract).then_inc(s_glo, 1)

        @block.tensor
        def _(pe):
            def turn(m, first):
                if not first:
                    pe.wait_ge(s_x0t, m)
                pe.wait_ge(s_block, m * 32 + 32)
                for d in range(D):
                    w = P if d == 0 else BLOCK_B
                    ins = nc.tensor.transpose(
                        side[0:XROWS, d * BLOCK_B:d * BLOCK_B + w],
                        emb_block[0:w, :, :].rearrange("b e (j d) -> b (e j) d", d=D)[:, :, d], ident[0:w, 0:w])
                ins.then_inc(s_side, 1)

            def turn_back(m):
                pe.wait_ge(s_x0, m + 1)
                for t in range(TILES):
                    ins = nc.tensor.transpose(side[:, t * XROWS:(t + 1) * XROWS], x0[:, t * P:(t + 1) * P],
                                              ident[0:XROWS, 0:XROWS])
                ins.then_inc(s_side, 1)

            def layer0(m, c, first):
                if c == 0 and not first:
                    pe.wait_ge(s_x1, m)
                w, start, stop = pairs(c), c == 0, c == PAIR_CHUNKS - 1
                if c in SPLIT:
                    i = SPLIT.index(c)
                    pe.wait_ge(s_qlo, len(SPLIT) * m + i + 1)
                    nc.tensor.matmul(x1_ps[:, :], w0_hi[0:w, i, :], quad_hi[0:w, :], start=start, stop=False)
                    nc.tensor.matmul(x1_ps[:, :], w0_lo[0:w, i, :], quad_hi[0:w, :], start=False, stop=False)
                    nc.tensor.matmul(x1_ps[:, :], w0_hi[0:w, i, :], quad_lo[0:w, c, :], start=False,
                                     stop=stop).then_inc(s_l0, 1)
                else:
                    pe.wait_ge(s_quad, PAIR_CHUNKS * m + c + 1)
                    nc.tensor.matmul(x1_ps[:, :], w0_t[0:w, WHOLE.index(c), :], quad[0:w, c, :], start=start,
                                     stop=stop).then_inc(s_l0, 1)

            def layer1(n, g, first):
                t, c = divmod(g, CHUNKS)
                if c == 0 and t in (0, TILES - 1):
                    pe.wait_ge(s_x1l, 2 * n + 1 + (t > 0))
                if not (first and g < VBANKS):
                    was = g - VBANKS
                    back = was < 0
                    was += SLOTS * back
                    if was % CHUNKS in DVE_CHUNKS:
                        pe.wait_ge(s_stt, n * (TILES * STT_TILE) + stt_done(was) - back * TILES * STT_TILE)
                    else:
                        pe.wait_ge(s_mul, n * (TILES * MUL_TILE) + mul_done(was) - back * TILES * MUL_TILE)
                w = len(FIELDS[c]) * H
                a = STARTS[c] * H
                hi, lo, out = x1_hi[:, t * P:(t + 1) * P], x1_lo[:, t * P:(t + 1) * P], v[:, g % VBANKS, 0:w]
                nc.tensor.matmul(out, hi, w1_hi[:, a:a + w], start=True, stop=False)
                nc.tensor.matmul(out, hi, w1_lo[:, a:a + w], start=False, stop=False)
                nc.tensor.matmul(out, lo, w1_hi[:, a:a + w], start=False, stop=True).then_inc(s_v, 1)

            def form_g2(n, t):
                if not (isinstance(n, int) and n == 0 and t == 0):
                    pe.wait_ge(s_g2e, n * TILES + t)
                pe.wait_ge(s_x2, (n * TILES + t + 1) * X2_TILE)
                nc.tensor.matmul(g2_ps[:, 0:TILE_B * FE], x2_t[:, t % 2, :], spread[:, t % 2, :], start=True,
                                 stop=True).then_inc(s_g2, 1)

            def step(n, first=False, last=False):
                for g in range(SLOTS):
                    layer1(n, g, first)
                    if not last:
                        m = n + 1
                        if g == S_TURN:
                            turn(m, False)
                        if g == S_BACK:
                            turn_back(m)
                        if g in L0_AT:
                            layer0(m, L0_AT.index(g), False)
                    for at in late(n, g, LAG_G2, first):
                        form_g2(*at)

            pe.wait_ge(s_const, 32)
            for s in range(GROUPS):
                if s >= VBANKS:
                    pe.wait_ge(s_tr_hi, s - VBANKS + 1)
                    if s - VBANKS >= 2:
                        pe.wait_ge(s_tr_lo, min(s - VBANKS - 1, LO_GROUPS))
                bank = v[:, s % VBANKS, :]
                if s < 3:
                    if s == 0:
                        pe.wait_ge(s_sym, 1)
                    for x, c in enumerate(W0_GROUPS[s]):
                        d0, d1 = PER_CHUNK * c, min(PER_CHUNK * c + PER_CHUNK, NDELTA)
                        ins = nc.tensor.transpose(bank[0:pairs(c), x * H:(x + 1) * H],
                                                  w0_sym[:, d0:d1, :].rearrange("h e j -> h (e j)"), ident[:, :])
                else:
                    raw, c, loaded = (w1_raw, s - W1_GROUP0, s_w1) if s < W2_GROUP0 else (w2_raw, s - W2_GROUP0, s_w2)
                    pe.wait_ge(loaded, 16)
                    for x, j in enumerate(FIELDS[c]):
                        ins = nc.tensor.transpose(bank[:, x * H:(x + 1) * H], raw[:, j * H:(j + 1) * H], ident[:, :])
                ins.then_inc(s_tr, 1)
            turn(0, True)
            turn_back(0)
            for c in range(PAIR_CHUNKS):
                layer0(0, c, True)
            pe.wait_ge(s_tr_hi, GROUPS)
            pe.wait_ge(s_tr_lo, LO_GROUPS)
            step(0, first=True)
            with pe.Fori(1, NBLOCKS - 1) as i:
                step(i)
            step(NBLOCKS - 1, last=True)
            pe.wait_ge(s_dense, 16)
            for t in range(BTILES):
                ins = nc.tensor.transpose(side[0:D, t * P:(t + 1) * P], dense_raw[:, t, :], ident[:, :])
            ins.then_inc(s_dense_t, 1)
            pe.wait_ge(s_top, 48)
            pe.wait_ge(s_z1, NBLOCKS)
            pe.wait_ge(s_mul, NBLOCKS * TILES * MUL_TILE)
            pe.wait_ge(s_stt, NBLOCKS * TILES * STT_TILE)
            for c in range(4):
                nc.tensor.matmul(v[:, 1 + c, :], wt1[:, 0, c * P:(c + 1) * P], z1[:, :], start=True, stop=False)
            for at in left(LAG_G2):
                form_g2(*at)
            pe.wait_ge(s_dense_t, 2)
            for c in range(4):
                nc.tensor.matmul(v[:, 1 + c, :], wt1_dense[:, c * P:(c + 1) * P], dense_t[:, :], start=False, stop=False)
            pe.wait_ge(s_g2e, NBLOCKS * TILES)
            pe.wait_ge(s_x1, NBLOCKS)
            for j in range(F):
                w, last = slice(j * H, (j + 1) * H), j == F - 1
                if j < PLAIN:
                    nc.tensor.matmul(x1_ps[:, :], w2_t[:, w], g2[:, j, :], start=(j == 0), stop=False).then_inc(s_z3, 1)
                else:
                    pe.wait_ge(s_w2lo, j // JC)
                    if j % JC == LO_POOL:
                        pe.wait_ge(s_glo_pool, j // JC)
                    else:
                        pe.wait_ge(s_glo, j - PLAIN + 1 - (j // JC - 1))
                    hi = g2_hi[:, j % HI_RING, :]
                    nc.tensor.matmul(x1_ps[:, :], w2_hi[:, w], hi, start=False, stop=False)
                    nc.tensor.matmul(x1_ps[:, :], w2_lo[:, w], hi, start=False, stop=False)
                    nc.tensor.matmul(x1_ps[:, :], w2_hi[:, w], g2_lo[:, j, :], start=False, stop=last).then_inc(s_z3, 1)
            for c in range(4):
                nc.tensor.matmul(v[:, 1 + c, :], wt1[:, 1, c * P:(c + 1) * P], g2[:, F, :], start=False, stop=False)
            pe.wait_ge(s_z3e, 1)
            for c in range(4):
                nc.tensor.matmul(v[:, 1 + c, :], wt1[:, 2, c * P:(c + 1) * P], z3[:, :], start=False,
                                 stop=True).then_inc(s_m1, 1)
            for k in range(4):
                pe.wait_ge(s_m1e, k + 1)
                for c in range(2):
                    ins = nc.tensor.matmul(top_ps[c][:, :], wt2[:, k, c * P:(c + 1) * P], h1[:, k, :], start=(k == 0),
                                           stop=(k == 3))
                    if k == 3:
                        ins.then_inc(s_m2, 1)
            for k in range(2):
                pe.wait_ge(s_m2e, k + 1)
                ins = nc.tensor.matmul(side[0:1, :], wt3[:, k:k + 1], h2[:, k, :], start=(k == 0), stop=(k == 1))
            ins.then_inc(s_y, 1)


def constants():
    ident = np.eye(P, dtype=np.float32)
    mask = np.zeros((P, TILE_B), np.float32)
    for p in range(P):
        mask[p, p // D] = 1.0
    return ident, mask


def kernel(**inputs):
    import concourse.bacc as bacc
    from concourse.bass_utils import run_bass_kernel_spmd as run

    nc = bacc.Bacc("TRN2", target_bir_lowering=False, num_devices=1)
    arrays = {}

    def given(name, a):
        a = np.ascontiguousarray(a)
        arrays[f"in_{name}_dram"] = a
        return nc.dram_tensor(f"in_{name}_dram", a.shape, mybir.dt.from_np(a.dtype), kind="ExternalInput").ap()

    ids = given("ids", inputs["ids"])
    tables = [given(f"tbl_{j}", inputs[f"tbl_{j}"]) for j in range(F)]
    rest = [given(k, inputs[k]) for k in ("dense_ctx", "W_top1", "b_top1", "W_top2", "b_top2", "W_top3",
                                          "L0_rec_W0", "L0_rec_b0", "L0_rec_W1", "L0_rec_b1",
                                          "L0_rec_W2", "L0_rec_b2")]
    fixed = [given(k, a) for k, a in zip(("ident", "mask"), constants())]
    y = nc.dram_tensor("out_y_dram", (B, 1), F32, kind="ExternalOutput").ap()
    bass_dlrm(nc, ids, tables, *rest, *fixed, y)
    r = run(nc, [arrays], core_ids=[0])
    return r.results[0]["out_y_dram"]
```
